# Optimizing a Trainium2 kernel written in Bass

```python
import numpy as np
import jax
import jax.numpy as jnp

def _softmax(x, axis=-1):
    return jax.nn.softmax(x, axis=axis)

def _gelu(x):
    return jax.nn.gelu(x, approximate=True)

def _silu(x):
    return jax.nn.silu(x)

def _sigmoid(x):
    return jax.nn.sigmoid(x)

def _layernorm(x, axis=-1, eps=1e-05):
    m = jnp.mean(x, axis=axis, keepdims=True)
    v = jnp.var(x, axis=axis, keepdims=True)
    return (x - m) / jnp.sqrt(v + eps)

def _scatter_add(tgt, idx, src, axis=0):
    return tgt.at[idx].add(src)

def _segment_sum(src, seg, n):
    return jax.ops.segment_sum(src, seg, n)
kernel_name = 'mk_adaln_d1_jaxref_r4_7e2388'

def setup_inputs(seed: int=0):
    np.random.seed(seed)
    _w = jnp.asarray

    def _L0_attn_setup():
        import jax, jax.numpy as jnp
        import numpy as np
        EMBED_DIM = 256
        NUM_HEADS = 16
        DEPTH = 12
        HEAD_DIM = EMBED_DIM // NUM_HEADS // 2
        LAMBDA_INIT = float(0.8 - 0.6 * np.exp(-0.3 * DEPTH))
        B, T = (2, 512)
        key = jax.random.key(seed)
        ks = jax.random.split(key, 10)
        s = 0.02
        return {'query': jax.random.normal(ks[0], (B, T, EMBED_DIM), jnp.float32), 'Wq': jax.random.normal(ks[1], (EMBED_DIM, EMBED_DIM), jnp.float32) * s, 'Wk': jax.random.normal(ks[2], (EMBED_DIM, EMBED_DIM), jnp.float32) * s, 'Wv': jax.random.normal(ks[3], (EMBED_DIM, EMBED_DIM), jnp.float32) * s, 'Wo': jax.random.normal(ks[4], (EMBED_DIM, EMBED_DIM), jnp.float32) * s, 'lambda_q1': jax.random.normal(ks[5], (HEAD_DIM,), jnp.float32) * 0.1, 'lambda_k1': jax.random.normal(ks[6], (HEAD_DIM,), jnp.float32) * 0.1, 'lambda_q2': jax.random.normal(ks[7], (HEAD_DIM,), jnp.float32) * 0.1, 'lambda_k2': jax.random.normal(ks[8], (HEAD_DIM,), jnp.float32) * 0.1, 'subln_w': jnp.ones((2 * HEAD_DIM,), jnp.float32)}
    _L0_attn_in = _L0_attn_setup()

    def _L0_ffn_setup():
        import jax, jax.numpy as jnp
        import numpy as np
        EPS = 1e-05

        @jax.custom_vjp
        def ste_quantize(w):
            scale = jnp.maximum(jnp.mean(jnp.abs(w)), EPS)
            return jnp.clip(jnp.round(w / scale), -1.0, 1.0)

        def _ste_fwd(w):
            return (ste_quantize(w), None)

        def _ste_bwd(_, g):
            return (g,)
        ste_quantize.defvjp(_ste_fwd, _ste_bwd)
        key = jax.random.key(seed)
        k1, k2 = jax.random.split(key)
        x = jax.random.normal(k1, (8, 2048, 256), dtype=jnp.float32)
        weight = jax.random.normal(k2, (256, 256), dtype=jnp.float32) * 0.02
        return {'x': x, 'weight': weight}
    _L0_ffn_in = _L0_ffn_setup()
    _L0_c = _w((lambda *s: np.random.randn(*s).astype(np.float32) * 0.05)(4, 256))
    _L0_wmod = _w((lambda *s: np.random.randn(*s).astype(np.float32) * 0.05)(256, 6 * 256) * 256 ** (-0.5))
    _d = {'L0_attn_query': _L0_attn_in['query'], 'L0_attn_Wq': _L0_attn_in['Wq'], 'L0_attn_Wk': _L0_attn_in['Wk'], 'L0_attn_Wv': _L0_attn_in['Wv'], 'L0_attn_Wo': _L0_attn_in['Wo'], 'L0_attn_lambda_q1': _L0_attn_in['lambda_q1'], 'L0_attn_lambda_k1': _L0_attn_in['lambda_k1'], 'L0_attn_lambda_q2': _L0_attn_in['lambda_q2'], 'L0_attn_lambda_k2': _L0_attn_in['lambda_k2'], 'L0_attn_subln_w': _L0_attn_in['subln_w'], 'L0_ffn_weight': _L0_ffn_in['weight'], 'L0_c': _L0_c, 'L0_wmod': _L0_wmod}
    _x0 = _d['L0_attn_query']
    _d['L0_attn_query'] = jax.random.normal(jax.random.fold_in(jax.random.key(seed), 1), (4, 2048, 256), dtype=_x0.dtype)
    del _x0
    return _d

def reference(L0_attn_query, L0_attn_Wq, L0_attn_Wk, L0_attn_Wv, L0_attn_Wo, L0_attn_lambda_q1, L0_attn_lambda_k1, L0_attn_lambda_q2, L0_attn_lambda_k2, L0_attn_subln_w, L0_ffn_weight, L0_c, L0_wmod):

    def _L0_attn_ref(query, Wq, Wk, Wv, Wo, lambda_q1, lambda_k1, lambda_q2, lambda_k2, subln_w):
        import jax, jax.numpy as jnp
        import numpy as np
        EMBED_DIM = 256
        NUM_HEADS = 16
        DEPTH = 12
        HEAD_DIM = EMBED_DIM // NUM_HEADS // 2
        LAMBDA_INIT = float(0.8 - 0.6 * np.exp(-0.3 * DEPTH))
        B, T = (2, 512)
        Bsz, Tt, E = query.shape
        H, hd = (NUM_HEADS, HEAD_DIM)
        scaling = hd ** (-0.5)
        q = jnp.einsum('bte,fe->btf', query, Wq).reshape(Bsz, Tt, 2 * H, hd).transpose(0, 2, 1, 3)
        k = jnp.einsum('bse,fe->bsf', query, Wk).reshape(Bsz, Tt, 2 * H, hd).transpose(0, 2, 1, 3)
        v = jnp.einsum('bse,fe->bsf', query, Wv).reshape(Bsz, Tt, H, 2 * hd).transpose(0, 2, 1, 3)
        q = q * scaling
        scores = jnp.einsum('bhtd,bhsd->bhts', q, k)
        attn_w = jax.nn.softmax(scores.astype(jnp.float32), axis=-1).astype(q.dtype)
        lam1 = jnp.exp(jnp.sum(lambda_q1 * lambda_k1))
        lam2 = jnp.exp(jnp.sum(lambda_q2 * lambda_k2))
        lam = lam1 - lam2 + LAMBDA_INIT
        aw = attn_w.reshape(Bsz, H, 2, Tt, Tt)
        aw = aw[:, :, 0] - lam * aw[:, :, 1]
        attn = jnp.einsum('bhts,bhsd->bhtd', aw, v)
        x32 = attn.astype(jnp.float32)
        normed = (x32 * jax.lax.rsqrt(jnp.mean(x32 * x32, axis=-1, keepdims=True) + 1e-05)).astype(attn.dtype)
        attn = normed * subln_w
        attn = attn * (1.0 - LAMBDA_INIT)
        out = attn.transpose(0, 2, 1, 3).reshape(Bsz, Tt, H * 2 * hd)
        return jnp.einsum('bte,fe->btf', out, Wo)

    def _L0_ffn_ref(x, weight):
        import jax, jax.numpy as jnp
        import numpy as np
        EPS = 1e-05

        @jax.custom_vjp
        def ste_quantize(w):
            scale = jnp.maximum(jnp.mean(jnp.abs(w)), EPS)
            return jnp.clip(jnp.round(w / scale), -1.0, 1.0)

        def _ste_fwd(w):
            return (ste_quantize(w), None)

        def _ste_bwd(_, g):
            return (g,)
        ste_quantize.defvjp(_ste_fwd, _ste_bwd)
        w_ternary = ste_quantize(weight)
        scale = jnp.maximum(jnp.mean(jnp.abs(weight)), EPS)
        return jnp.einsum('bsi,oi->bso', x, w_ternary * scale)
    x = L0_attn_query
    mod = (_silu(L0_c) @ L0_wmod).reshape(L0_c.shape[0], 6, 1, -1)
    sa, ca, ga, sb, cb, gb = (mod[:, 0], mod[:, 1], mod[:, 2], mod[:, 3], mod[:, 4], mod[:, 5])
    ga = (2 * (ga >= 0) - 1) * jnp.maximum(jnp.abs(ga), 0.25)
    gb = (2 * (gb >= 0) - 1) * jnp.maximum(jnp.abs(gb), 0.25)
    h = _layernorm(x, axis=-1) * (1 + ca) + sa
    x = x + ga * _L0_attn_ref(h, L0_attn_Wq, L0_attn_Wk, L0_attn_Wv, L0_attn_Wo, L0_attn_lambda_q1, L0_attn_lambda_k1, L0_attn_lambda_q2, L0_attn_lambda_k2, L0_attn_subln_w)
    h = _layernorm(x, axis=-1) * (1 + cb) + sb
    x = x + gb * _L0_ffn_ref(h, L0_ffn_weight)
    return x

_drawn_inputs = setup_inputs


def setup_inputs(seed=0):
    import zlib

    import numpy as np

    out = dict(_drawn_inputs(seed))
    spreads = {'L0_attn_subln_w': (1.0, 0.6)}
    factors = {'L0_attn_Wq': 4.673,
     'L0_attn_Wk': 4.588,
     'L0_attn_Wv': 4.17,
     'L0_attn_Wo': 4.221,
     'L0_attn_lambda_q1': 8.0,
     'L0_attn_lambda_k1': 8.0,
     'L0_attn_lambda_q2': 8.0,
     'L0_attn_lambda_k2': 8.0}
    for name, (base, spread) in spreads.items():
        noise = np.random.default_rng([zlib.crc32(name.encode()), seed]).standard_normal(out[name].shape)
        drawn = base * np.exp(spread * noise) if base else spread * noise
        out[name] = jnp.asarray(drawn.astype(out[name].dtype))
    for name, factor in factors.items():
        out[name] = (out[name] * factor).astype(out[name].dtype)
    return out
```

```python
from contextlib import ExitStack

import numpy as np

import concourse.bass as bass
from concourse import mybir

ALU = mybir.AluOpType
ACT = mybir.ActivationFunctionType
AX = mybir.AxisListType
F32 = mybir.dt.float32
BF16 = mybir.dt.bfloat16
P = 128


def wait_alone(eng, sem, value, passed):
    eng.wait_ge(sem, value)
    eng.sem_inc(passed, 1)


class Chain:

    def __init__(self, eng, sem, start, passed=None):
        self.eng, self.sem, self.start, self.count, self.passed = eng, sem, start, 0, passed

    def then(self, instruction):
        self.count += 1
        instruction.then_inc(self.sem, 1)
        self.eng.wait_ge(self.sem, self.start + self.count)
        if self.passed:
            self.eng.sem_inc(self.passed, 1)


def adaln_diff_attention(nc, x, wqT, wkT, wvT, woT, lq1, lk1, lq2, lk2, subln, wfT, cT, wmod, out):
    B, T, E = x.shape
    HD = lq1.shape[0]
    VD = 2 * HD
    NH = E // VD
    NS = 2 * NH
    NG = NS // 4
    CH = 512
    NC = T // CH
    NB = T // P
    BPC = CH // P
    EC = E // P
    PAIRS = 2
    SLOTS = 3
    PRING = 4
    LAG = 2
    VW = 32
    PARTS = 3
    UNITS = NC * NB
    BODY = 2 * UNITS
    SEGS = 2 * NC
    GP = NG // 2
    assert GP == NC
    QK_ROWS = [(0, 0), (0, 1), (1, 0), (1, 1), (0, 2), (2, 0)]
    KQ = HD * len(QK_ROWS)
    KS_ROWS = KQ + PARTS
    LAMBDA_INIT = float(0.8 - 0.6 * np.exp(-0.3 * 12))
    SCALING = float(np.float32(HD ** -0.5))
    EPS = 1e-5
    A_STEPS, E_STEPS = 8, 6
    S_LINKS, E_LINKS = 7, 6
    GROUP_LOADS = 2 * 2 * len(QK_ROWS) + 2 + 1
    ROW_LOADS = 2 * 2 * len(QK_ROWS)
    DMA = 16

    q_scr = nc.dram_tensor("q_scr", [B, PARTS, E, T], BF16, kind="Internal").ap()
    k_scr = nc.dram_tensor("k_scr", [B, PARTS, E, T], BF16, kind="Internal").ap()
    v_scr = nc.dram_tensor("v_scr", [B, NG, P, NB, 2 * VW], F32, kind="Internal").ap()
    m_scr = nc.dram_tensor("m_scr", [B, PARTS, NS, T], BF16, kind="Internal").ap()
    attn_scr = nc.dram_tensor("attn_scr", [B, E, T], F32, kind="Internal").ap()
    mod_scr = nc.dram_tensor("mod_scr", [B, 6, E], F32, kind="Internal").ap()

    with ExitStack() as ctx:
        def sb(name, shape, dt=F32):
            return ctx.enter_context(nc.sbuf_tensor(name, shape, dt))

        def sem(name):
            return ctx.enter_context(nc.semaphore(name))

        ident = sb("ident", [P, P])
        ones = sb("ones", [P, P])
        neg_half = sb("neg_half", [P, 16])
        wq, wk, wv, wo, wf = (sb(f"w_{n}", [P, EC, E]) for n in ("q", "k", "v", "o", "f"))
        wmod_sb = sb("wmod_sb", [P, EC, 6 * E])
        c_sb = sb("c_sb", [P, EC, B])
        c_exp = sb("c_exp", [P, EC, B])
        silu = sb("silu", [P, EC, B])
        mod_sb = sb("mod_sb", [B, 6, E])
        gate_abs = sb("gate_abs", [B, E])
        gate_sign = sb("gate_sign", [B, E])
        w_sum = sb("w_sum", [P, 1])
        w_scale = sb("w_scale", [P, 1])
        w_half = sb("w_half", [P, 2])
        w_low = sb("w_low", [P, EC, E])
        lam_in = sb("lam_in", [P, 4, HD])
        lam_prod = sb("lam_prod", [P, 2, HD])
        lam_sum = sb("lam_sum", [P, 2])
        lam_exp = sb("lam_exp", [P, 2])
        coef = sb("coef", [P, 1])
        subln_sb = sb("subln_sb", [2 * 32, VD])
        keys = [sb(f"keys{i}", [P, PAIRS, T], BF16) for i in range(2)]
        queries = [sb(f"queries{i}", [P, PAIRS, T], BF16) for i in range(2)]
        values = [sb(f"values{i}", [P, NB, 2, VW]) for i in range(2)]
        probs = sb("probs", [P, PRING, PAIRS, 2, CH])
        seg_t = sb("seg_t", [P, CH // 32, 32])
        seg_r = sb("seg_r", [P, CH // 32])
        seg_rc = sb("seg_rc", [P, CH // 32])
        seg_w = sb("seg_w", [P, CH // 32, VD])
        seg_w2 = sb("seg_w2", [64, CH // 32, VD])
        seg_d = sb("seg_d", [64, CH // 32, VD])
        seg_sq = sb("seg_sq", [64, CH // 32, VD])
        seg_ss = sb("seg_ss", [64, CH // 32])
        seg_ms = sb("seg_ms", [64, CH // 32])
        seg_rs = sb("seg_rs", [64, CH // 32])
        seg_n = sb("seg_n", [64, CH // 32, VD])
        seg_a = sb("seg_a", [32, CH // 32, 2 * VD])
        seg_o = sb("seg_o", [32, CH])
        a_x = sb("a_x", [P, BPC, E])
        a_cols = sb("a_cols", [P, 2, EC])
        stats = sb("stats", [P, BPC, 6])
        moments = sb("moments", [P, BPC, 2])
        a_ve = sb("a_ve", [P, BPC])
        a_rstd = sb("a_rstd", [P, BPC])
        normed = sb("normed", [P, BPC, E])
        a_hT = sb("a_hT", [P, EC, CH])
        a_qk = sb("a_qk", [P, 4, CH])
        a_rest = sb("a_rest", [P, CH])
        a_parts = sb("a_parts", [P, 4, PARTS, CH], BF16)
        a_v = sb("a_v", [P, NG, BPC, 2, VW])
        e_attn = sb("e_attn", [P, EC, CH])
        e_x = sb("e_x", [P, BPC, E])
        e_cols = sb("e_cols", [P, 2, EC])
        e_gate = sb("e_gate", [P, 2, E])
        e_open_t = sb("e_open_t", [P, 1])
        e_tmp = sb("e_tmp", [P, 2, E])
        e_x2 = sb("e_x2", [P, BPC, E])
        e_ve = sb("e_ve", [P, BPC])
        e_rstd = sb("e_rstd", [P, BPC])
        e_hT = sb("e_hT", [P, EC, CH])
        e_y = sb("e_y", [P, BPC, E])
        m_cols = sb("m_cols", [P, NB, NS])
        m_rows = sb("m_rows", [NS, T])
        m_parts = sb("m_parts", [NS, PARTS, T], BF16)

        ps = ctx.enter_context(nc.psum_tensor("ps", [P, 8, 512], F32))
        slots = [ps[:, 2 * s:2 * s + 2, :] for s in range(SLOTS)]
        pv = ps[:, 6, :]
        aux = ps[:, 7, :]

        sp_passed, pool_passed, pe_passed, dve_passed = (sem(f"{e}_passed") for e in ("sp", "pool", "pe", "dve"))
        consts_set = sem("consts_set")
        ident_set = sem("ident_set")
        weights_loaded = sem("weights_loaded")
        small_loaded = sem("small_loaded")
        c_exp_done = sem("c_exp_done")
        start_chain = sem("start_chain")
        silu_done = sem("silu_done")
        mod_product = sem("mod_product")
        mod_done = sem("mod_done")
        mod_stored = sem("mod_stored")
        w_sum_done = sem("w_sum_done")
        w_total = sem("w_total")
        setup_done = sem("setup_done")
        lam_sum_done = sem("lam_sum_done")
        lam_exp_done = sem("lam_exp_done")
        a_loaded = sem("a_loaded")
        a_var = sem("a_var")
        a_rstd_done = sem("a_rstd_done")
        a_normed = sem("a_normed")
        a_product = sem("a_product")
        a_evacuated = sem("a_evacuated")
        a_split = sem("a_split")
        a_pool_chain = sem("a_pool_chain")
        a_chain = sem("a_chain")
        a_stored = sem("a_stored")
        e_loaded = sem("e_loaded")
        e_open = sem("e_open")
        e_product = sem("e_product")
        e_evacuated = sem("e_evacuated")
        e_var = sem("e_var")
        e_rstd_done = sem("e_rstd_done")
        e_normed = sem("e_normed")
        e_chain = sem("e_chain")
        e_stored = sem("e_stored")
        m_open = sem("m_open")
        m_rows_loaded = sem("m_rows_loaded")
        m_scores = sem("m_scores")
        m_reduced = sem("m_reduced")
        m_transposed = sem("m_transposed")
        m_chain = sem("m_chain")
        m_done = sem("m_done")
        m_stored = sem("m_stored")
        group_loaded = [sem(f"group_loaded{i}") for i in range(2)]
        scores_ready = sem("scores_ready")
        exp_done = sem("exp_done")
        pv_done = sem("pv_done")
        pv_read = sem("pv_read")
        s_chain = sem("s_chain")
        s_chain_n = sem("s_chain_n")
        seg_ms_done = sem("seg_ms_done")
        seg_rs_done = sem("seg_rs_done")
        seg_done = sem("seg_done")
        seg_stored = sem("seg_stored")

        block = ctx.enter_context(nc.Block())

        @block.sync
        def _(sp):
            for name, w, src in (("q", wq, wqT), ("k", wk, wkT), ("v", wv, wvT), ("o", wo, woT), ("f", wf, wfT)):
                sp.dma_start(w[:, :, :], src.rearrange("(c p) f -> p c f", p=P)).then_inc(weights_loaded, DMA)
            sp.dma_start(wmod_sb[:, :, :], wmod.rearrange("(c p) f -> p c f", p=P)).then_inc(weights_loaded, DMA)
            sp.dma_start(c_sb[:, :, :], cT.rearrange("(c p) b -> p c b", p=P)).then_inc(small_loaded, DMA)
            for i, v in enumerate((lq1, lk1, lq2, lk2)):
                sp.dma_start(lam_in[:, i, :], v.rearrange("(o d) -> o d", o=1).broadcast_to([P, HD])).then_inc(small_loaded, DMA)
            sp.dma_start(subln_sb[:, :], subln.rearrange("(o d) -> o d", o=1).broadcast_to([64, VD])).then_inc(small_loaded, DMA)
            sp.wait_ge(mod_done, 1)
            sp.dma_start(mod_scr, mod_sb[:, :, :]).then_inc(mod_stored, DMA)
            sp.wait_ge(mod_stored, DMA)

            def inside(value, most, why):
                return nc.s_assert_within(value, 0, most, skip_runtime_bounds_check_because=why)

            def a_loads(b, tc):
                sp.dma_start(a_x[:, :, :], x[bass.ds(b, 1), bass.ds(tc * CH, CH), :].rearrange("o (n p) e -> p (o n) e", p=P)).then_inc(a_loaded, DMA)
                for c in range(EC):
                    sp.dma_start(a_cols[:, :, c], mod_scr[bass.ds(b, 1), 0:2, c * P:(c + 1) * P].rearrange("o k p -> p (o k)"), allow_slow_non_contiguous=True).then_inc(a_loaded, DMA)

            def a_store_qk(job, b, tc, i):
                wait_alone(sp, a_split, job * 4 + i + 1, sp_passed)
                dst = (q_scr, k_scr)[i // 2]
                c = i % 2
                sp.dma_start(dst[bass.ds(b, 1), :, c * P:(c + 1) * P, bass.ds(tc * CH, CH)].rearrange("o s p t -> p (o s) t"),
                             a_parts[:, i, :, :]).then_inc(a_stored, DMA)

            def a_store_v(job, b, tc):
                sp.wait_ge(a_evacuated, (job + 1) * A_STEPS)
                for g in range(NG):
                    sp.dma_start(v_scr[bass.ds(b, 1), g, :, bass.ds(tc * BPC, BPC), :].rearrange("o p n w -> p (o n) w"),
                                 a_v[:, g, :, :, :].rearrange("p n h w -> p n (h w)")).then_inc(a_stored, DMA)

            def a_wait(job):
                wait_alone(sp, a_stored, (job + 1) * (4 + NG) * DMA, sp_passed)

            def e_loads(b, tc):
                for c in range(EC):
                    sp.dma_start(e_attn[:, c, :], attn_scr[bass.ds(b, 1), c * P:(c + 1) * P, bass.ds(tc * CH, CH)].rearrange("o p t -> p (o t)")).then_inc(e_loaded, DMA)
                sp.dma_start(e_x[:, :, :], x[bass.ds(b, 1), bass.ds(tc * CH, CH), :].rearrange("o (n p) e -> p (o n) e", p=P)).then_inc(e_loaded, DMA)
                for c in range(EC):
                    sp.dma_start(e_cols[:, :, c], mod_scr[bass.ds(b, 1), 3:5, c * P:(c + 1) * P].rearrange("o k p -> p (o k)"), allow_slow_non_contiguous=True).then_inc(e_loaded, DMA)
                for i, kind in enumerate((2, 5)):
                    sp.dma_start(e_gate[:, i, :], mod_scr[bass.ds(b, 1), kind, :].broadcast_to([P, E])).then_inc(e_loaded, DMA)

            def e_store(job, b, tc):
                sp.wait_ge(e_evacuated, (job + 1) * E_STEPS)
                sp.dma_start(out[bass.ds(b, 1), bass.ds(tc * CH, CH), :].rearrange("o (n p) e -> p (o n) e", p=P), e_y[:, :, :]).then_inc(e_stored, DMA)
                wait_alone(sp, e_stored, (job + 1) * DMA, sp_passed)

            def rows_of(b, g, buf, loaded):
                for half in range(2):
                    for r, (qp, kp) in enumerate(QK_ROWS):
                        at = 64 * half + HD * r
                        for tile, scr, part in ((queries[buf], q_scr, qp), (keys[buf], k_scr, kp)):
                            src = scr[bass.ds(b, 1), part, bass.ds(g * 4 * HD + half * 2 * HD, 2 * HD), :]
                            sp.dma_start(tile[at:at + HD, :, :], src.rearrange("o (s d) t -> d (o s) t", d=HD)).then_inc(loaded, DMA)

            def group_loads(b, g, buf):
                rows_of(b, g, buf, group_loaded[buf])
                for half in range(2):
                    at = 64 * half + KQ
                    src = m_scr[bass.ds(b, 1), :, bass.ds(g * 4 + half * 2, 2), :]
                    sp.dma_start(queries[buf][at:at + PARTS, :, :], src.rearrange("o i s t -> (o i) s t")).then_inc(group_loaded[buf], DMA)
                src = v_scr[bass.ds(b, 1), bass.ds(g, 1), :, :, :]
                sp.dma_start(values[buf][:, :, :, :].rearrange("p n h w -> p n (h w)"),
                             src.rearrange("o u p n w -> p (o u n) w")).then_inc(group_loaded[buf], DMA)

            with sp.Fori(0, NC) as tc:
                a_loads(0, tc)
                for i in range(4):
                    a_store_qk(tc, 0, tc, i)
                a_store_v(tc, 0, tc)
                a_wait(tc)

            with sp.Fori(0, B) as b:
                with sp.Fori(0, NG) as g:
                    rows_of(b, g, 0, m_rows_loaded)
                    wait_alone(sp, m_scores, (b * NG + g + 1) * (4 * NB), sp_passed)
                sp.wait_ge(m_done, b + 1)
                sp.dma_start(m_scr[bass.ds(b, 1), :, :, :].rearrange("o i s t -> s (o i) t"), m_parts[:, :, :]).then_inc(m_stored, DMA)
                sp.wait_ge(m_stored, (b + 1) * DMA)
                group_loads(b, 0, 0)
                with sp.Fori(0, GP) as gp:
                    body = b * GP + gp
                    ejob = (body + (B - 1) * GP) % (B * GP)
                    group_loads(b, gp * 2 + 1, 1)
                    after, before = (b + 1) % B, (b + B - 1) % B
                    with sp.If(b < B - 1):
                        a_loads(after, gp)
                    with sp.If(b > 0):
                        e_loads(before, gp)
                    for s in range(SEGS):
                        if s in (1, 2):
                            with sp.If(b < B - 1):
                                a_store_qk(body + NC, after, gp, 2 * (s - 1))
                                a_store_qk(body + NC, after, gp, 2 * (s - 1) + 1)
                        if s == 3:
                            with sp.If(b < B - 1):
                                a_store_v(body + NC, after, gp)
                        if s == 7:
                            with sp.If(b > 0):
                                e_store(ejob, before, gp)
                            with sp.If(b < B - 1):
                                a_wait(body + NC)
                        sp.wait_ge(seg_done, body * SEGS + s + 1)
                        sp.dma_start(attn_scr[bass.ds(b, 1), bass.ds((gp * 2 + s // NC) * 32, 32), (s % NC) * CH:(s % NC + 1) * CH].rearrange("o p t -> p (o t)"),
                                     seg_o[:, :]).then_inc(seg_stored, DMA)
                        if s == NC:
                            with sp.If(gp < GP - 1):
                                sp.wait_ge(pv_done, body * BODY + UNITS)
                                group_loads(b, inside(gp * 2 + 2, NG - 1, "inside If(gp < GP - 1)"), 0)
                    wait_alone(sp, seg_stored, (body + 1) * SEGS * DMA, sp_passed)

            with sp.Fori(0, NC) as tc:
                e_loads(B - 1, tc)
                e_store((B - 1) * NC + tc, B - 1, tc)

        @block.gpsimd
        def _(pool):
            nc.gpsimd.memset(ones[:, :], 1.0).then_inc(consts_set, 1)
            nc.gpsimd.memset(neg_half[:, :], -0.5).then_inc(consts_set, 1)
            nc.gpsimd.memset(ident[:, :], 0.0).then_inc(ident_set, 1)
            pool.wait_ge(ident_set, 1)
            nc.gpsimd.affine_select(out=ident[:, :], in_=ident[:, :], compare_op=ALU.not_equal, fill=1.0, base=0,
                                    pattern=[[-1, P]], channel_multiplier=1).then_inc(ident_set, 1)
            for buf in range(2):
                nc.gpsimd.memset(keys[buf][:, :, :], 1.0).then_inc(consts_set, 1)
            nc.gpsimd.memset(a_v[:, :, :, :, :], 0.0).then_inc(consts_set, 1)
            pool.wait_ge(consts_set, 5)
            nc.gpsimd.memset(a_v[:, :, :, :, VD:VD + 1], 1.0).then_inc(consts_set, 1)

            def a_power(job):
                pool.wait_ge(a_var, job + 1)
                nc.gpsimd.tensor_tensor(a_rstd[:, :], a_ve[:, :], neg_half[:, 0:BPC], ALU.pow).then_inc(a_rstd_done, 1)

            def a_split_parts(job, i):
                src = a_qk[:, i, :]
                link = Chain(pool, a_pool_chain, job * 12 + i * 3, pool_passed)
                wait_alone(pool, a_evacuated, job * A_STEPS + 3 + i, pool_passed)
                link.then(nc.gpsimd.tensor_copy(a_parts[:, i, 0, :], src))
                link.then(nc.gpsimd.tensor_tensor(a_rest[:, :], src, a_parts[:, i, 0, :], ALU.subtract))
                link.then(nc.gpsimd.tensor_copy(a_parts[:, i, 1, :], a_rest[:, :]))
                nc.gpsimd.tensor_tensor(a_parts[:, i, 2, :], a_rest[:, :], a_parts[:, i, 1, :], ALU.subtract).then_inc(a_split, 1)
                wait_alone(pool, a_split, job * 4 + i + 1, pool_passed)

            def e_power(job):
                pool.wait_ge(e_var, job + 1)
                nc.gpsimd.tensor_tensor(e_rstd[:, :], e_ve[:, :], neg_half[:, 0:BPC], ALU.pow).then_inc(e_rstd_done, 1)

            with pool.Fori(0, NC) as tc:
                a_power(tc)
                for i in range(4):
                    a_split_parts(tc, i)
            with pool.Fori(0, B) as b:
                with pool.Fori(0, GP) as gp:
                    body = b * GP + gp
                    ejob = (body + (B - 1) * GP) % (B * GP)
                    with pool.If(b < B - 1):
                        a_power(body + NC)
                    for s in range(SEGS):
                        if s in (1, 2):
                            with pool.If(b < B - 1):
                                a_split_parts(body + NC, 2 * (s - 1))
                                a_split_parts(body + NC, 2 * (s - 1) + 1)
                        if s == A_STEPS // 2:
                            with pool.If(b > 0):
                                e_power(ejob)
                        pool.wait_ge(seg_ms_done, body * SEGS + s + 1)
                        nc.gpsimd.tensor_tensor(seg_rs[:, :], seg_ms[:, :], neg_half[0:64, :], ALU.pow).then_inc(seg_rs_done, 1)
            with pool.Fori(0, NC) as tc:
                e_power((B - 1) * NC + tc)

        @block.scalar
        def _(act):
            act.wait_ge(small_loaded, 6 * DMA)
            nc.scalar.activation(c_exp[:, :, :], c_sb[:, :, :], ACT.Exp, scale=-1.0).then_inc(c_exp_done, 1)
            act.wait_ge(lam_sum_done, 1)
            nc.scalar.activation(lam_exp[:, :], lam_sum[:, :], ACT.Exp).then_inc(lam_exp_done, 1)
            with act.Fori(0, B * GP) as body:
                for n in range(2 * BODY):
                    u = n // PAIRS
                    act.wait_ge(scores_ready, body * (2 * BODY) + n + 1)
                    if n % PAIRS == 0 and u >= PRING:
                        act.wait_ge(pv_done, body * BODY + u - PRING + 1)
                    nc.scalar.activation(probs[:, u % PRING, n % PAIRS, :, :], slots[n % SLOTS], ACT.Exp).then_inc(exp_done, 1)

        @block.tensor
        def _(pe):
            pe.wait_ge(weights_loaded, 6 * DMA)
            pe.wait_ge(silu_done, 1)
            for k in range(3):
                for c in range(EC):
                    last = nc.tensor.matmul(ps[0:B, k, :], silu[:, c, :], wmod_sb[:, c, k * 512:(k + 1) * 512], start=(c == 0), stop=(c == EC - 1))
            last.then_inc(mod_product, 1)
            pe.wait_ge(w_sum_done, 1)
            pe.wait_ge(consts_set, 6)
            nc.tensor.matmul(ps[:, 3, 0:1], ones[:, :], w_sum[:, :], start=True, stop=True).then_inc(w_total, 1)
            pe.wait_ge(ident_set, 2)
            pe.wait_ge(setup_done, 1)

            def transposes(src, c):
                for n in range(BPC):
                    last = nc.tensor.transpose(aux[:, n * P:(n + 1) * P], src[:, n, c * P:(c + 1) * P], ident[:, :])
                return last

            def token_products(hT, w, n0):
                for n in range(n0, n0 + 2):
                    for c in range(EC):
                        last = nc.tensor.matmul(aux[:, (n - n0) * E:(n - n0 + 1) * E], hT[:, c, n * P:(n + 1) * P], w[:, c, :],
                                                start=(c == 0), stop=(c == EC - 1))
                return last

            def a_step(job, i):
                if i == 0:
                    pe.wait_ge(a_normed, job + 1)
                else:
                    pe.wait_ge(a_evacuated, job * A_STEPS + i)
                if i < 2:
                    last = transposes(normed, i)
                elif i < 6:
                    w = (wq, wk)[(i - 2) // 2]
                    f = (i - 2) % 2
                    for c in range(EC):
                        last = nc.tensor.matmul(aux, w[:, c, f * P:(f + 1) * P], a_hT[:, c, :], start=(c == 0), stop=(c == EC - 1))
                else:
                    last = token_products(a_hT, wv, (i - 6) * 2)
                last.then_inc(a_product, 1)

            def e_step(job, i):
                if i == 0:
                    pe.wait_ge(e_loaded, (job + 1) * 7 * DMA)
                    pe.wait_ge(e_open, job + 1)
                else:
                    pe.wait_ge(e_evacuated, job * E_STEPS + i)
                if i < 2:
                    last = token_products(e_attn, wo, i * 2)
                elif i < 4:
                    pe.wait_ge(e_normed, job + 1)
                    last = transposes(normed, i - 2)
                else:
                    last = token_products(e_hT, wf, (i - 4) * 2)
                last.then_inc(e_product, 1)

            def scores(body, u, n):
                buf, tc, blk = u // UNITS, u // NB % NC, u % NB
                if n >= SLOTS:
                    pe.wait_ge(exp_done, body * (2 * BODY) + n - SLOTS + 1)
                for half in range(2):
                    at = 64 * half
                    last = nc.tensor.matmul(slots[n % SLOTS][:, half, :], keys[buf][at:at + KS_ROWS, n % PAIRS, blk * P:(blk + 1) * P],
                                            queries[buf][at:at + KS_ROWS, n % PAIRS, tc * CH:(tc + 1) * CH], start=True, stop=True)
                last.then_inc(scores_ready, 1)

            def weighted(body, u):
                buf, blk, seg = u // UNITS, u % NB, u // NB
                if blk == 0:
                    pe.wait_ge(pv_read, body * SEGS + seg + 1)
                pe.wait_ge(exp_done, body * (2 * BODY) + PAIRS * (u + 1))
                for pair in range(PAIRS):
                    for half in range(2):
                        j = 32 * (2 * pair + half)
                        last = nc.tensor.matmul(pv[j:j + VW, :], values[buf][:, blk, half, :], probs[:, u % PRING, pair, half, :],
                                                start=(blk == 0), stop=(blk == NB - 1))
                last.then_inc(pv_done, 1)

            with pe.Fori(0, NC) as tc:
                for i in range(A_STEPS):
                    a_step(tc, i)

            with pe.Fori(0, B) as b:
                wait_alone(pe, m_open, b + 1, pe_passed)
                with pe.Fori(0, NG) as g:
                    pe.wait_ge(m_rows_loaded, (b * NG + g + 1) * (ROW_LOADS * DMA))
                    for n in range(4 * NB):
                        head, blk = n // NB, n % NB
                        pair, at = head // 2, 64 * (head % 2)
                        pe.wait_ge(m_reduced, (b * NG + g) * (4 * NB) + n + 1)
                        for k in range(NC):
                            last = nc.tensor.matmul(ps[:, 4 * (n % 2) + k, :], queries[0][at:at + KQ, pair, blk * P:(blk + 1) * P],
                                                    keys[0][at:at + KQ, pair, k * CH:(k + 1) * CH], start=True, stop=True)
                        last.then_inc(m_scores, 1)
                pe.wait_ge(m_reduced, (b + 1) * NG * (4 * NB) + 2)
                for blk in range(NB):
                    last = nc.tensor.transpose(ps[0:NS, blk // BPC, (blk % BPC) * P:(blk % BPC + 1) * P], m_cols[:, blk, :], ident[:, :])
                last.then_inc(m_transposed, 1)
                wait_alone(pe, m_done, b + 1, pe_passed)

                with pe.Fori(0, GP) as gp:
                    body = b * GP + gp
                    ejob = (body + (B - 1) * GP) % (B * GP)
                    for u in range(BODY + LAG):
                        if u < BODY:
                            if u % UNITS == 0:
                                buf = u // UNITS
                                pe.wait_ge(group_loaded[buf], (body + 1) * (GROUP_LOADS * DMA))
                            for n in (PAIRS * u, PAIRS * u + 1):
                                scores(body, u, n)
                        if u >= LAG:
                            weighted(body, u - LAG)
                        if u % 8 == 0 and u >= 8:
                            i = u // 8 - 1
                            if i < A_STEPS:
                                with pe.If(b < B - 1):
                                    a_step(body + NC, i)
                            elif i < A_STEPS + E_STEPS:
                                with pe.If(b > 0):
                                    e_step(ejob, i - A_STEPS)

            with pe.Fori(0, NC) as tc:
                for i in range(E_STEPS):
                    e_step((B - 1) * NC + tc, i)

        @block.vector
        def _(dve):
            V = nc.vector
            link = Chain(dve, start_chain, 0)
            dve.wait_ge(c_exp_done, 1)
            link.then(V.tensor_scalar(c_exp[:, :, :], c_exp[:, :, :], 1.0, None, ALU.add))
            link.then(V.reciprocal(c_exp[:, :, :], c_exp[:, :, :]))
            V.tensor_tensor(silu[:, :, :], c_sb[:, :, :], c_exp[:, :, :], ALU.mult).then_inc(silu_done, 1)
            lam4 = lam_in[:, :, :].rearrange("p (i j) d -> p i j d", j=2)
            link.then(V.tensor_tensor(lam_prod[:, :, :], lam4[:, :, 0, :], lam4[:, :, 1, :], ALU.mult))
            V.tensor_reduce(lam_sum[:, :], lam_prod[:, :, :], axis=AX.X, op=ALU.add).then_inc(lam_sum_done, 1)
            dve.wait_ge(weights_loaded, 6 * DMA)
            V.tensor_reduce(w_sum[:, :], wf[:, :, :], axis=AX.XY, op=ALU.add, apply_absolute_value=True).then_inc(w_sum_done, 1)
            dve.wait_ge(lam_exp_done, 1)
            link.then(V.tensor_scalar(coef[:, :], lam_exp[:, 1:2], lam_exp[:, 0:1], -LAMBDA_INIT, ALU.subtract, ALU.add))
            link.then(V.memset(coef[0:64, :], 1.0))
            dve.wait_ge(mod_product, 1)
            link.then(V.tensor_copy(mod_sb[:, :, :].rearrange("b k e -> b (k e)"), ps[0:B, 0:3, :].rearrange("b k e -> b (k e)")))
            for kind in (1, 4):
                V.tensor_scalar(mod_sb[:, kind, :], mod_sb[:, kind, :], 1.0, None, ALU.add)
            for kind in (2, 5):
                link.then(V.scalar_tensor_tensor(gate_abs[:, :], mod_sb[:, kind, :], -1.0, mod_sb[:, kind, :], ALU.mult, ALU.max))
                V.tensor_scalar(gate_abs[:, :], gate_abs[:, :], 0.25, None, ALU.max)
                link.then(V.tensor_scalar(gate_sign[:, :], mod_sb[:, kind, :], 0.0, 2.0, ALU.is_ge, ALU.mult))
                link.then(V.scalar_tensor_tensor(mod_sb[:, kind, :], gate_sign[:, :], -1.0, gate_abs[:, :], ALU.add, ALU.mult))
            V.tensor_copy(e_open_t[0:B, :], mod_sb[:, 0, 0:1]).then_inc(mod_done, 1)
            dve.wait_ge(w_total, 1)
            link.then(V.tensor_scalar(w_scale[:, :], ps[:, 3, 0:1], 1.0 / (E * E), 1e-5, ALU.mult, ALU.max))
            V.tensor_scalar(w_half[:, 0:1], w_scale[:, :], 0.5, None, ALU.mult)
            link.then(V.tensor_scalar(w_half[:, 1:2], w_scale[:, :], -0.5, None, ALU.mult))
            V.tensor_scalar(w_low[:, :, :], wf[:, :, :], w_half[:, 1:2], w_scale[:, :], ALU.is_lt, ALU.mult)
            link.then(V.tensor_scalar(wf[:, :, :], wf[:, :, :], w_half[:, 0:1], w_scale[:, :], ALU.is_gt, ALU.mult))
            link.then(V.tensor_tensor(wf[:, :, :], wf[:, :, :], w_low[:, :, :], ALU.subtract))
            V.memset(e_open_t[:, :], 0.0).then_inc(pv_read, 1)
            link.then(V.memset(seg_r[:, :], 0.0))
            V.memset(seg_rc[:, :], 0.0).then_inc(m_reduced, 2)
            V.memset(stats[:, 0, :], 0.0).then_inc(setup_done, 1)
            dve.wait_ge(setup_done, 1)

            def norm(link, src, ve, rstd, var_sem, rstd_sem, job, done):
                for n in range(BPC):
                    last = V.bn_stats(stats[:, n, :], src[:, n, :])
                link.then(last)
                dve.sem_inc(dve_passed, 1)
                for n in range(BPC):
                    last = V.bn_aggr(moments[:, n, :], stats[:, n, :])
                link.then(last)
                V.tensor_scalar(ve[:, :], moments[:, :, 1], EPS, None, ALU.add).then_inc(var_sem, 1)
                dve.wait_ge(rstd_sem, job + 1)
                for n in range(BPC):
                    last = V.tensor_scalar(normed[:, n, :], src[:, n, :], moments[:, n, 0:1], rstd[:, n:n + 1], ALU.subtract, ALU.mult)
                last.then_inc(done, 1)

            def a_norm(job):
                dve.wait_ge(a_loaded, (job + 1) * 3 * DMA)
                norm(Chain(dve, a_chain, job * 2), a_x, a_ve, a_rstd, a_var, a_rstd_done, job, a_normed)

            def a_evacuate(job, i):
                dve.wait_ge(a_product, job * A_STEPS + i + 1)
                if i < 2:
                    last = V.tensor_scalar(a_hT[:, i, :], aux, a_cols[:, 1, i:i + 1], a_cols[:, 0, i:i + 1], ALU.mult, ALU.add)
                elif i < 6:
                    last = V.tensor_scalar(a_qk[:, i - 2, :], aux, SCALING if i < 4 else 1.0, None, ALU.mult)
                else:
                    for n in range(2):
                        last = V.tensor_copy(a_v[:, :, (i - 6) * 2 + n, :, 0:VD], aux[:, n * E:(n + 1) * E].rearrange("p (g h d) -> p g h d", g=NG, h=2))
                last.then_inc(a_evacuated, 1)

            def e_evacuate(job, i):
                if i == 0:
                    dve.wait_ge(e_loaded, (job + 1) * 7 * DMA)
                    V.tensor_copy(e_open_t[:, :], e_cols[:, 0, 0:1]).then_inc(e_open, 1)
                link = Chain(dve, e_chain, job * E_LINKS + (0, 1, 4, 4, 4, 5)[i])
                dve.wait_ge(e_product, job * E_STEPS + i + 1)
                two = aux.rearrange("p (n e) -> p n e", n=2)
                n0 = (i % 2) * 2
                if i in (2, 3):
                    V.tensor_scalar(e_hT[:, i - 2, :], aux, e_cols[:, 1, i - 2:i - 1], e_cols[:, 0, i - 2:i - 1], ALU.mult, ALU.add).then_inc(e_evacuated, 1)
                    return
                gate, base, dst = (0, e_x, e_x2) if i < 2 else (1, e_x2, e_y)
                link.then(V.tensor_tensor(e_tmp[:, :, :], two, e_gate[:, gate:gate + 1, :].broadcast_to([P, 2, E]), ALU.mult))
                V.tensor_tensor(dst[:, n0:n0 + 2, :], e_tmp[:, :, :], base[:, n0:n0 + 2, :], ALU.add).then_inc(e_evacuated, 1)
                wait_alone(dve, e_evacuated, job * E_STEPS + i + 1, dve_passed)
                if i == 1:
                    norm(link, e_x2, e_ve, e_rstd, e_var, e_rstd_done, job, e_normed)

            def segment(body, s):
                NQ = CH // 32
                link = Chain(dve, s_chain, (body * SEGS + s) * S_LINKS)
                if s:
                    wait_alone(dve, seg_stored, (body * SEGS + s) * DMA, dve_passed)
                else:
                    with dve.If(body > 0):
                        wait_alone(dve, seg_stored, body * (SEGS * DMA), dve_passed)
                dve.wait_ge(pv_done, body * BODY + (s + 1) * NB)
                V.transpose(seg_t[:, :, :].rearrange("p c d -> p (c d)"), pv).then_inc(pv_read, 1)
                dve.wait_ge(pv_read, body * SEGS + s + 2)
                link.then(V.reciprocal(seg_r[:, :], seg_t[:, :, VD]))
                link.then(V.tensor_scalar(seg_rc[:, :], seg_r[:, :], coef[:, 0:1], None, ALU.mult))
                link.then(V.tensor_tensor(seg_w[:, :, :], seg_t[:, :, 0:VD], seg_rc[:, :].rearrange("p (c o) -> p c o", o=1).broadcast_to([P, NQ, VD]), ALU.mult))
                link.then(V.tensor_copy(seg_w2[:, :, :], seg_w[64:128, :, :]))
                link.then(V.tensor_tensor(seg_d[:, :, :], seg_w[0:64, :, :], seg_w2[:, :, :], ALU.add))
                link.then(V.tensor_tensor(seg_sq[:, :, :], seg_d[:, :, :], seg_d[:, :, :], ALU.mult))
                link.then(V.tensor_reduce(seg_ss[0:64, :], seg_sq[:, :, :], axis=AX.X, op=ALU.add))
                V.tensor_scalar(seg_ms[:, :], seg_ss[0:64, :], 1.0 / VD, EPS, ALU.mult, ALU.add).then_inc(seg_ms_done, 1)
                dve.wait_ge(seg_rs_done, body * SEGS + s + 1)
                V.tensor_tensor(seg_n[:, :, :], seg_d[:, :, :], seg_rs[:, :].rearrange("p (c o) -> p c o", o=1).broadcast_to([64, NQ, VD]), ALU.mult).then_inc(s_chain_n, 1)
                dve.wait_ge(s_chain_n, (body * SEGS + s) * 2 + 1)
                for h in range(2):
                    q = slice(32 * h, 32 * h + 32)
                    last = V.scalar_tensor_tensor(seg_a[:, :, h * VD:(h + 1) * VD], seg_n[q, :, :], 1.0 - LAMBDA_INIT,
                                                  subln_sb[q, :].rearrange("p (o d) -> p o d", o=1).broadcast_to([32, NQ, VD]), ALU.mult, ALU.mult)
                last.then_inc(s_chain_n, 1)
                dve.wait_ge(s_chain_n, (body * SEGS + s) * 2 + 2)
                V.transpose(seg_o[:, :], seg_a[:, :, :].rearrange("p c d -> p (c d)")).then_inc(seg_done, 1)

            with dve.Fori(0, NC) as tc:
                a_norm(tc)
                for i in range(A_STEPS):
                    a_evacuate(tc, i)

            with dve.Fori(0, B) as b:
                V.memset(e_open_t[:, :], 0.0).then_inc(m_open, 1)
                with dve.Fori(0, NG) as g:
                    for n in range(4 * NB):
                        head, blk = n // NB, n % NB
                        shead = 2 * (head % 2) + head // 2
                        dve.wait_ge(m_scores, (b * NG + g) * (4 * NB) + n + 1)
                        V.tensor_reduce(m_cols[:, blk, bass.ds(g * 4 + shead, 1)], ps[:, 4 * (n % 2):4 * (n % 2) + 4, :], axis=AX.XY, op=ALU.max).then_inc(m_reduced, 1)
                dve.wait_ge(m_transposed, b + 1)
                link = Chain(dve, m_chain, b * 4)
                link.then(V.tensor_scalar(m_rows[:, :], ps[0:NS, 0:4, :].rearrange("p a b -> p (a b)"), -1.0, None, ALU.mult))
                link.then(V.tensor_copy(m_parts[:, 0, :], m_rows[:, :]))
                link.then(V.tensor_tensor(m_rows[:, :], m_rows[:, :], m_parts[:, 0, :], ALU.subtract))
                link.then(V.tensor_copy(m_parts[:, 1, :], m_rows[:, :]))
                V.tensor_tensor(m_parts[:, 2, :], m_rows[:, :], m_parts[:, 1, :], ALU.subtract).then_inc(m_done, 1)

                with dve.Fori(0, GP) as gp:
                    body = b * GP + gp
                    ejob = (body + (B - 1) * GP) % (B * GP)
                    with dve.If(b < B - 1):
                        a_norm(body + NC)
                    for s in range(SEGS):
                        for i in (2 * s, 2 * s + 1):
                            if i < A_STEPS:
                                with dve.If(b < B - 1):
                                    a_evacuate(body + NC, i)
                            elif i < A_STEPS + E_STEPS:
                                with dve.If(b > 0):
                                    e_evacuate(ejob, i - A_STEPS)
                        segment(body, s)

            with dve.Fori(0, NC) as tc:
                for i in range(E_STEPS):
                    e_evacuate((B - 1) * NC + tc, i)


_OUTS = [((4, 2048, 256), "float32")]


def kernel(**inputs):
    import concourse.bacc as _bacc
    from concourse.bass_utils import run_bass_kernel_spmd as _run

    nc = _bacc.Bacc("TRN2", target_bir_lowering=False, num_devices=1)
    plain = {k: np.asarray(v) for k, v in inputs.items()}
    laid = [
        ("x", plain["L0_attn_query"]),
        ("wqT", plain["L0_attn_Wq"].T), ("wkT", plain["L0_attn_Wk"].T), ("wvT", plain["L0_attn_Wv"].T), ("woT", plain["L0_attn_Wo"].T),
        ("lq1", plain["L0_attn_lambda_q1"]), ("lk1", plain["L0_attn_lambda_k1"]),
        ("lq2", plain["L0_attn_lambda_q2"]), ("lk2", plain["L0_attn_lambda_k2"]),
        ("subln", plain["L0_attn_subln_w"]), ("wfT", plain["L0_ffn_weight"].T),
        ("cT", plain["L0_c"].T), ("wmod", plain["L0_wmod"]),
    ]
    arrays, args = {}, []
    for name, a in laid:
        a = np.ascontiguousarray(a)
        arrays[f"in_{name}_dram"] = a
        args.append(nc.dram_tensor(f"in_{name}_dram", a.shape, mybir.dt.from_np(a.dtype), kind="ExternalInput").ap())
    for i, (shape, dtype) in enumerate(_OUTS):
        args.append(nc.dram_tensor(f"out_{i}_dram", shape, mybir.dt.from_np(np.dtype(dtype)), kind="ExternalOutput").ap())
    adaln_diff_attention(nc, *args)
    r = _run(nc, [arrays], core_ids=[0])
    return r.results[0]["out_0_dram"]
```

```python
from contextlib import ExitStack

import numpy as np

import concourse.bass as bass
from concourse import mybir

ALU = mybir.AluOpType
ACT = mybir.ActivationFunctionType
AX = mybir.AxisListType
F32 = mybir.dt.float32
BF16 = mybir.dt.bfloat16
P = 128


def wait_alone(eng, sem, value, passed):
    eng.wait_ge(sem, value)
    eng.sem_inc(passed, 1)


class Chain:

    def __init__(self, eng, sem, start, passed=None):
        self.eng, self.sem, self.start, self.count, self.passed = eng, sem, start, 0, passed

    def then(self, instruction):
        self.count += 1
        instruction.then_inc(self.sem, 1)
        self.eng.wait_ge(self.sem, self.start + self.count)
        if self.passed:
            self.eng.sem_inc(self.passed, 1)


def adaln_diff_attention(nc, x, wqT, wkT, wvT, woT, lq1, lk1, lq2, lk2, subln, wfT, cT, wmod, out):
    B, T, E = x.shape
    HD = lq1.shape[0]
    VD = 2 * HD
    NH = E // VD
    NS = 2 * NH
    NG = NS // 4
    CH = 512
    NC = T // CH
    NB = T // P
    BPC = CH // P
    EC = E // P
    PAIRS = 2
    SLOTS = 3
    PRING = 4
    LAG = 2
    VW = 32
    PARTS = 3
    UNITS = NC * NB
    BODY = 2 * UNITS
    SEGS = 2 * NC
    GP = NG // 2
    assert GP == NC
    QK_ROWS = [(0, 0), (0, 1), (1, 0), (1, 1), (0, 2), (2, 0)]
    KQ = HD * len(QK_ROWS)
    KS_ROWS = 64
    BOX = NC + 1
    HEADROOM = 20.0
    MAX_SLACK = 80.0
    MAX_SIZE = 256.0
    LAMBDA_INIT = float(0.8 - 0.6 * np.exp(-0.3 * 12))
    SCALING = float(np.float32(HD ** -0.5))
    EPS = 1e-5
    A_STEPS, E_STEPS = 8, 6
    STEP_UNITS = [NB * (n // 2) + (9, 13)[n % 2] for n in range(A_STEPS + E_STEPS)]
    S_LINKS, E_LINKS, M_LINKS = 7, 6, 14
    GROUP_LOADS = 2 * 2 * len(QK_ROWS) + 2 + 1
    ROW_LOADS = 2 * 2 * len(QK_ROWS)
    DMA = 16

    q_scr = nc.dram_tensor("q_scr", [B, PARTS, E, T], BF16, kind="Internal").ap()
    k_scr = nc.dram_tensor("k_scr", [B, PARTS, E, T], BF16, kind="Internal").ap()
    v_scr = nc.dram_tensor("v_scr", [B, NG, P, NB, 2 * VW], F32, kind="Internal").ap()
    m_scr = nc.dram_tensor("m_scr", [B, PARTS, NS, T], BF16, kind="Internal").ap()
    attn_scr = nc.dram_tensor("attn_scr", [B, E, T], F32, kind="Internal").ap()
    mod_scr = nc.dram_tensor("mod_scr", [B, 6, E], F32, kind="Internal").ap()

    with ExitStack() as ctx:
        def sb(name, shape, dt=F32):
            return ctx.enter_context(nc.sbuf_tensor(name, shape, dt))

        def sem(name):
            return ctx.enter_context(nc.semaphore(name))

        ident = sb("ident", [P, P])
        ones = sb("ones", [P, P])
        neg_half = sb("neg_half", [P, 16])
        wq, wk, wv, wo, wf = (sb(f"w_{n}", [P, EC, E]) for n in ("q", "k", "v", "o", "f"))
        wmod_sb = sb("wmod_sb", [P, EC, 6 * E])
        c_sb = sb("c_sb", [P, EC, B])
        c_exp = sb("c_exp", [P, EC, B])
        silu = sb("silu", [P, EC, B])
        mod_sb = sb("mod_sb", [B, 6, E])
        gate_abs = sb("gate_abs", [B, E])
        gate_sign = sb("gate_sign", [B, E])
        w_sum = sb("w_sum", [P, 1])
        w_scale = sb("w_scale", [P, 1])
        w_half = sb("w_half", [P, 2])
        w_low = sb("w_low", [P, EC, E])
        lam_in = sb("lam_in", [P, 4, HD])
        lam_prod = sb("lam_prod", [P, 2, HD])
        lam_sum = sb("lam_sum", [P, 2])
        lam_exp = sb("lam_exp", [P, 2])
        coef = sb("coef", [P, 1])
        subln_sb = sb("subln_sb", [2 * 32, VD])
        keys = [sb(f"keys{i}", [P, PAIRS, T], BF16) for i in range(2)]
        queries = [sb(f"queries{i}", [P, PAIRS, T], BF16) for i in range(2)]
        values = [sb(f"values{i}", [P, NB, 2, VW]) for i in range(2)]
        probs = sb("probs", [P, PRING, PAIRS, 2, CH])
        seg_t = sb("seg_t", [P, CH // 32, 32])
        seg_r = sb("seg_r", [P, CH // 32])
        seg_rc = sb("seg_rc", [P, CH // 32])
        seg_w = sb("seg_w", [P, CH // 32, VD])
        seg_w2 = sb("seg_w2", [64, CH // 32, VD])
        seg_d = sb("seg_d", [64, CH // 32, VD])
        seg_sq = sb("seg_sq", [64, CH // 32, VD])
        seg_ss = sb("seg_ss", [64, CH // 32])
        seg_ms = sb("seg_ms", [64, CH // 32])
        seg_rs = sb("seg_rs", [64, CH // 32])
        seg_n = sb("seg_n", [64, CH // 32, VD])
        seg_a = sb("seg_a", [32, CH // 32, 2 * VD])
        seg_o = sb("seg_o", [32, CH])
        a_x = sb("a_x", [P, BPC, E])
        a_cols = sb("a_cols", [P, 2, EC])
        stats = sb("stats", [P, BPC, 6])
        moments = sb("moments", [P, BPC, 2])
        a_ve = sb("a_ve", [P, BPC])
        a_rstd = sb("a_rstd", [P, BPC])
        normed = sb("normed", [P, BPC, E])
        a_hT = sb("a_hT", [P, EC, CH])
        a_qk = sb("a_qk", [P, 4, CH])
        a_rest = sb("a_rest", [P, CH])
        a_sum = sb("a_sum", [P, EC, NC])
        a_qabs = sb("a_qabs", [P, EC, NC])
        box = sb("box", [P, EC, 2, BOX])
        q_sign = sb("q_sign", [P, EC, 2, T], BF16)
        a_parts = sb("a_parts", [P, 4, PARTS, CH], BF16)
        a_v = sb("a_v", [P, NG, BPC, 2, VW])
        e_attn = sb("e_attn", [P, EC, CH])
        e_x = sb("e_x", [P, BPC, E])
        e_cols = sb("e_cols", [P, 2, EC])
        e_gate = sb("e_gate", [P, 2, E])
        e_open_t = sb("e_open_t", [P, 1])
        e_tmp = sb("e_tmp", [P, 2, E])
        e_x2 = sb("e_x2", [P, BPC, E])
        e_ve = sb("e_ve", [P, BPC])
        e_rstd = sb("e_rstd", [P, BPC])
        e_hT = sb("e_hT", [P, EC, CH])
        e_y = sb("e_y", [P, BPC, E])
        head_mask = sb("head_mask", [P, NS // EC])
        box_w = sb("box_w", [P, EC, 2, NS // EC, BOX], BF16)
        m_mean = sb("m_mean", [P, EC])
        m_size = sb("m_size", [P, 4, EC])
        m_slack = sb("m_slack", [P, NB * NS])
        m_crit = sb("m_crit", [P, 3])
        m_worst = sb("m_worst", [1, 1])
        m_flag = sb("m_flag", [1, 1], mybir.dt.int32)
        m_cols = sb("m_cols", [P, NB, NS])
        m_rows = probs[0:NS, 0, :, :, :].rearrange("p a b t -> p (a b t)")
        m_parts = wmod_sb[0:NS, :, :].rearrange("p c f -> p (c f)").bitcast(BF16).rearrange("p (i t) -> p i t", i=PARTS)

        ps = ctx.enter_context(nc.psum_tensor("ps", [P, 8, 512], F32))
        slots = [ps[:, 2 * s:2 * s + 2, :] for s in range(SLOTS)]
        pv = ps[:, 6, :]
        aux = ps[:, 7, :]

        sp_passed, pool_passed, pe_passed, dve_passed = (sem(f"{e}_passed") for e in ("sp", "pool", "pe", "dve"))
        consts_set = sem("consts_set")
        ident_set = sem("ident_set")
        weights_loaded = sem("weights_loaded")
        small_loaded = sem("small_loaded")
        c_exp_done = sem("c_exp_done")
        start_chain = sem("start_chain")
        silu_done = sem("silu_done")
        mod_product = sem("mod_product")
        mod_done = sem("mod_done")
        mod_stored = sem("mod_stored")
        w_sum_done = sem("w_sum_done")
        w_total = sem("w_total")
        setup_done = sem("setup_done")
        lam_sum_done = sem("lam_sum_done")
        lam_exp_done = sem("lam_exp_done")
        a_loaded = sem("a_loaded")
        a_var = sem("a_var")
        a_rstd_done = sem("a_rstd_done")
        a_normed = sem("a_normed")
        a_product = sem("a_product")
        a_evacuated = sem("a_evacuated")
        a_bounded = sem("a_bounded")
        a_split = sem("a_split")
        a_pool_chain = sem("a_pool_chain")
        a_chain = sem("a_chain")
        a_stored = sem("a_stored")
        e_loaded = sem("e_loaded")
        e_open = sem("e_open")
        e_product = sem("e_product")
        e_evacuated = sem("e_evacuated")
        e_var = sem("e_var")
        e_rstd_done = sem("e_rstd_done")
        e_normed = sem("e_normed")
        e_chain = sem("e_chain")
        e_stored = sem("e_stored")
        m_open = sem("m_open")
        m_rows_loaded = sem("m_rows_loaded")
        m_scores = sem("m_scores")
        m_reduced = sem("m_reduced")
        m_transposed = sem("m_transposed")
        m_bounds = sem("m_bounds")
        m_crit_done = sem("m_crit_done")
        m_crit_row = sem("m_crit_row")
        m_flag_set = sem("m_flag_set")
        m_chain = sem("m_chain")
        m_done = sem("m_done")
        m_stored = sem("m_stored")
        group_loaded = [sem(f"group_loaded{i}") for i in range(2)]
        scores_ready = sem("scores_ready")
        exp_done = sem("exp_done")
        pv_done = sem("pv_done")
        pv_read = sem("pv_read")
        s_chain = sem("s_chain")
        s_chain_n = sem("s_chain_n")
        seg_ms_done = sem("seg_ms_done")
        seg_rs_done = sem("seg_rs_done")
        seg_done = sem("seg_done")
        seg_stored = sem("seg_stored")

        block = ctx.enter_context(nc.Block())

        @block.sync
        def _(sp):
            for name, w, src in (("q", wq, wqT), ("k", wk, wkT), ("v", wv, wvT), ("o", wo, woT), ("f", wf, wfT)):
                sp.dma_start(w[:, :, :], src.rearrange("(c p) f -> p c f", p=P)).then_inc(weights_loaded, DMA)
            sp.dma_start(wmod_sb[:, :, :], wmod.rearrange("(c p) f -> p c f", p=P)).then_inc(weights_loaded, DMA)
            sp.dma_start(c_sb[:, :, :], cT.rearrange("(c p) b -> p c b", p=P)).then_inc(small_loaded, DMA)
            for i, v in enumerate((lq1, lk1, lq2, lk2)):
                sp.dma_start(lam_in[:, i, :], v.rearrange("(o d) -> o d", o=1).broadcast_to([P, HD])).then_inc(small_loaded, DMA)
            sp.dma_start(subln_sb[:, :], subln.rearrange("(o d) -> o d", o=1).broadcast_to([64, VD])).then_inc(small_loaded, DMA)
            sp.wait_ge(mod_done, 1)
            sp.dma_start(mod_scr, mod_sb[:, :, :]).then_inc(mod_stored, DMA)
            sp.wait_ge(mod_stored, DMA)

            def inside(value, most, why):
                return nc.s_assert_within(value, 0, most, skip_runtime_bounds_check_because=why)

            def a_loads(b, tc):
                sp.dma_start(a_x[:, :, :], x[bass.ds(b, 1), bass.ds(tc * CH, CH), :].rearrange("o (n p) e -> p (o n) e", p=P)).then_inc(a_loaded, DMA)
                for c in range(EC):
                    sp.dma_start(a_cols[:, :, c], mod_scr[bass.ds(b, 1), 0:2, c * P:(c + 1) * P].rearrange("o k p -> p (o k)"), allow_slow_non_contiguous=True).then_inc(a_loaded, DMA)

            def a_store_qk(job, b, tc, i):
                wait_alone(sp, a_split, job * 4 + i + 1, sp_passed)
                dst = (q_scr, k_scr)[i // 2]
                c = i % 2
                sp.dma_start(dst[bass.ds(b, 1), :, c * P:(c + 1) * P, bass.ds(tc * CH, CH)].rearrange("o s p t -> p (o s) t"),
                             a_parts[:, i, :, :]).then_inc(a_stored, DMA)

            def a_store_v(job, b, tc):
                sp.wait_ge(a_evacuated, (job + 1) * A_STEPS)
                for g in range(NG):
                    sp.dma_start(v_scr[bass.ds(b, 1), g, :, bass.ds(tc * BPC, BPC), :].rearrange("o p n w -> p (o n) w"),
                                 a_v[:, g, :, :, :].rearrange("p n h w -> p n (h w)")).then_inc(a_stored, DMA)

            def a_wait(job):
                wait_alone(sp, a_stored, (job + 1) * (4 + NG) * DMA, sp_passed)

            def e_loads(b, tc):
                for c in range(EC):
                    sp.dma_start(e_attn[:, c, :], attn_scr[bass.ds(b, 1), c * P:(c + 1) * P, bass.ds(tc * CH, CH)].rearrange("o p t -> p (o t)")).then_inc(e_loaded, DMA)
                sp.dma_start(e_x[:, :, :], x[bass.ds(b, 1), bass.ds(tc * CH, CH), :].rearrange("o (n p) e -> p (o n) e", p=P)).then_inc(e_loaded, DMA)
                for c in range(EC):
                    sp.dma_start(e_cols[:, :, c], mod_scr[bass.ds(b, 1), 3:5, c * P:(c + 1) * P].rearrange("o k p -> p (o k)"), allow_slow_non_contiguous=True).then_inc(e_loaded, DMA)
                for i, kind in enumerate((2, 5)):
                    sp.dma_start(e_gate[:, i, :], mod_scr[bass.ds(b, 1), kind, :].broadcast_to([P, E])).then_inc(e_loaded, DMA)

            def e_store(job, b, tc):
                sp.wait_ge(e_evacuated, (job + 1) * E_STEPS)
                sp.dma_start(out[bass.ds(b, 1), bass.ds(tc * CH, CH), :].rearrange("o (n p) e -> p (o n) e", p=P), e_y[:, :, :]).then_inc(e_stored, DMA)
                wait_alone(sp, e_stored, (job + 1) * DMA, sp_passed)

            def rows_of(b, g, buf, loaded):
                for half in range(2):
                    for r, (qp, kp) in enumerate(QK_ROWS):
                        at = 64 * half + HD * r
                        for tile, scr, part in ((queries[buf], q_scr, qp), (keys[buf], k_scr, kp)):
                            src = scr[bass.ds(b, 1), part, bass.ds(g * 4 * HD + half * 2 * HD, 2 * HD), :]
                            sp.dma_start(tile[at:at + HD, :, :], src.rearrange("o (s d) t -> d (o s) t", d=HD)).then_inc(loaded, DMA)

            def group_rows(b, g, buf):
                rows_of(b, g, buf, group_loaded[buf])
                src = v_scr[bass.ds(b, 1), bass.ds(g, 1), :, :, :]
                sp.dma_start(values[buf][:, :, :, :].rearrange("p n h w -> p n (h w)"),
                             src.rearrange("o u p n w -> p (o u n) w")).then_inc(group_loaded[buf], DMA)

            def group_maxima(b, g, buf):
                for half in range(2):
                    at = 64 * half + KQ
                    src = m_scr[bass.ds(b, 1), :, bass.ds(g * 4 + half * 2, 2), :]
                    sp.dma_start(queries[buf][at:at + PARTS, :, :], src.rearrange("o i s t -> (o i) s t")).then_inc(group_loaded[buf], DMA)

            with sp.Fori(0, NC) as tc:
                a_loads(0, tc)
                for i in range(4):
                    a_store_qk(tc, 0, tc, i)
                a_store_v(tc, 0, tc)
                a_wait(tc)
            group_rows(0, 0, 0)
            a_loads(1, 0)
            exact_runs = sp.alloc_register("sp_exact_runs")
            sp.reg_mov(exact_runs, 0)

            with sp.Fori(0, B) as b:
                wait_alone(sp, m_flag_set, b + 1, sp_passed)
                exact = sp.value_load(m_flag[0:1, 0:1], min_val=0, max_val=1)
                with sp.If(exact > 0):
                    runs = sp.snap(exact_runs, min_val=0, max_val=B - 1)
                    wait_alone(sp, group_loaded[0], (b * GP + 1) * ((GROUP_LOADS) * DMA) - 2 * DMA, sp_passed)
                    with sp.Fori(0, NG) as g:
                        rows_of(b, g, 0, m_rows_loaded)
                        wait_alone(sp, m_scores, (runs * NG + g + 1) * (4 * NB), sp_passed)
                    rows_of(b, 0, 0, m_rows_loaded)
                    wait_alone(sp, m_rows_loaded, (runs + 1) * ((NG + 1) * ROW_LOADS * DMA), sp_passed)
                    sp.reg_add(exact_runs, exact_runs, 1)
                sp.wait_ge(m_done, b + 1)
                sp.dma_start(m_scr[bass.ds(b, 1), :, :, :].rearrange("o i s t -> s (o i) t"), m_parts[:, :, :]).then_inc(m_stored, DMA)
                sp.wait_ge(m_stored, (b + 1) * DMA)
                group_maxima(b, 0, 0)
                with sp.Fori(0, GP) as gp:
                    body = b * GP + gp
                    ejob = (body + (B - 1) * GP) % (B * GP)
                    after, before = (b + 1) % B, (b + B - 1) % B
                    group_rows(b, gp * 2 + 1, 1)
                    group_maxima(b, gp * 2 + 1, 1)
                    with sp.If(b > 0):
                        e_loads(before, gp)
                    for s in range(SEGS):
                        if s in (1, 2):
                            with sp.If(b < B - 1):
                                a_store_qk(body + NC, after, gp, 2 * (s - 1))
                                a_store_qk(body + NC, after, gp, 2 * (s - 1) + 1)
                        if s == 3:
                            with sp.If(b < B - 1):
                                a_store_v(body + NC, after, gp)
                        if s == 7:
                            with sp.If(b > 0):
                                e_store(ejob, before, gp)
                            with sp.If(b < B - 1):
                                a_wait(body + NC)
                                with sp.If(gp < GP - 1):
                                    a_loads(after, inside(gp + 1, NC - 1, "inside If(gp < GP - 1)"))
                            with sp.If(b < B - 2):
                                with sp.If(gp == GP - 1):
                                    a_loads((b + 2) % B, 0)
                        sp.wait_ge(seg_done, body * SEGS + s + 1)
                        sp.dma_start(attn_scr[bass.ds(b, 1), bass.ds((gp * 2 + s // NC) * 32, 32), (s % NC) * CH:(s % NC + 1) * CH].rearrange("o p t -> p (o t)"),
                                     seg_o[:, :]).then_inc(seg_stored, DMA)
                        if s == NC:
                            with sp.If(gp < GP - 1):
                                sp.wait_ge(pv_done, body * BODY + UNITS)
                                g = inside(gp * 2 + 2, NG - 1, "inside If(gp < GP - 1)")
                                group_rows(b, g, 0)
                                group_maxima(b, g, 0)
                wait_alone(sp, seg_stored, (b + 1) * (GP * SEGS * DMA), sp_passed)
                with sp.If(b < B - 1):
                    group_rows((b + 1) % B, 0, 0)

            with sp.Fori(0, NC) as tc:
                e_loads(B - 1, tc)
                e_store((B - 1) * NC + tc, B - 1, tc)

        @block.gpsimd
        def _(pool):
            nc.gpsimd.memset(ones[:, :], 1.0).then_inc(consts_set, 1)
            nc.gpsimd.memset(neg_half[:, :], -0.5).then_inc(consts_set, 1)
            nc.gpsimd.memset(ident[:, :], 0.0).then_inc(ident_set, 1)
            pool.wait_ge(ident_set, 1)
            nc.gpsimd.affine_select(out=ident[:, :], in_=ident[:, :], compare_op=ALU.not_equal, fill=1.0, base=0,
                                    pattern=[[-1, P]], channel_multiplier=1).then_inc(ident_set, 1)
            for buf in range(2):
                nc.gpsimd.memset(keys[buf][:, :, :], 1.0).then_inc(consts_set, 1)
                nc.gpsimd.memset(queries[buf][:, :, :], 0.0).then_inc(consts_set, 1)
            nc.gpsimd.memset(head_mask[:, :], 1.0).then_inc(ident_set, 1)
            pool.wait_ge(ident_set, 3)
            nc.gpsimd.affine_select(out=head_mask[:, :], in_=head_mask[:, :], compare_op=ALU.is_ge, fill=0.0, base=0,
                                    pattern=[[-HD, NS // EC]], channel_multiplier=1).then_inc(ident_set, 1)
            pool.wait_ge(ident_set, 4)
            nc.gpsimd.affine_select(out=head_mask[:, :], in_=head_mask[:, :], compare_op=ALU.is_ge, fill=0.0, base=HD - 1,
                                    pattern=[[HD, NS // EC]], channel_multiplier=-1).then_inc(ident_set, 1)
            nc.gpsimd.memset(a_v[:, :, :, :, :], 0.0).then_inc(consts_set, 1)
            pool.wait_ge(consts_set, 7)
            nc.gpsimd.memset(a_v[:, :, :, :, VD:VD + 1], 1.0).then_inc(consts_set, 1)

            def a_power(job):
                pool.wait_ge(a_var, job + 1)
                nc.gpsimd.tensor_tensor(a_rstd[:, :], a_ve[:, :], neg_half[:, 0:BPC], ALU.pow).then_inc(a_rstd_done, 1)

            def a_split_parts(job, i):
                src = a_qk[:, i, :]
                link = Chain(pool, a_pool_chain, job * 12 + i * 3, pool_passed)
                wait_alone(pool, a_evacuated, job * A_STEPS + 3 + i, pool_passed)
                link.then(nc.gpsimd.tensor_copy(a_parts[:, i, 0, :], src))
                link.then(nc.gpsimd.tensor_tensor(a_rest[:, :], src, a_parts[:, i, 0, :], ALU.subtract))
                link.then(nc.gpsimd.tensor_copy(a_parts[:, i, 1, :], a_rest[:, :]))
                nc.gpsimd.tensor_tensor(a_parts[:, i, 2, :], a_rest[:, :], a_parts[:, i, 1, :], ALU.subtract).then_inc(a_split, 1)
                wait_alone(pool, a_split, job * 4 + i + 1, pool_passed)

            def e_power(job):
                pool.wait_ge(e_var, job + 1)
                nc.gpsimd.tensor_tensor(e_rstd[:, :], e_ve[:, :], neg_half[:, 0:BPC], ALU.pow).then_inc(e_rstd_done, 1)

            with pool.Fori(0, NC) as tc:
                a_power(tc)
                for i in range(4):
                    a_split_parts(tc, i)
            with pool.Fori(0, B) as b:
                with pool.Fori(0, GP) as gp:
                    body = b * GP + gp
                    ejob = (body + (B - 1) * GP) % (B * GP)
                    with pool.If(b < B - 1):
                        a_power(body + NC)
                    for s in range(SEGS):
                        if s in (1, 2):
                            with pool.If(b < B - 1):
                                a_split_parts(body + NC, 2 * (s - 1))
                                a_split_parts(body + NC, 2 * (s - 1) + 1)
                        if s == A_STEPS // 2:
                            with pool.If(b > 0):
                                e_power(ejob)
                        pool.wait_ge(seg_ms_done, body * SEGS + s + 1)
                        nc.gpsimd.tensor_tensor(seg_rs[:, :], seg_ms[:, :], neg_half[0:64, :], ALU.pow).then_inc(seg_rs_done, 1)
            with pool.Fori(0, NC) as tc:
                e_power((B - 1) * NC + tc)

        @block.scalar
        def _(act):
            act.wait_ge(small_loaded, 6 * DMA)
            nc.scalar.activation(c_exp[:, :, :], c_sb[:, :, :], ACT.Exp, scale=-1.0).then_inc(c_exp_done, 1)
            act.wait_ge(lam_sum_done, 1)
            nc.scalar.activation(lam_exp[:, :], lam_sum[:, :], ACT.Exp).then_inc(lam_exp_done, 1)
            with act.Fori(0, B * GP) as body:
                for n in range(2 * BODY):
                    u = n // PAIRS
                    act.wait_ge(scores_ready, body * (2 * BODY) + n + 1)
                    if n % PAIRS == 0 and u >= PRING:
                        act.wait_ge(pv_done, body * BODY + u - PRING + 1)
                    nc.scalar.activation(probs[:, u % PRING, n % PAIRS, :, :], slots[n % SLOTS], ACT.Exp).then_inc(exp_done, 1)

        @block.tensor
        def _(pe):
            pe.wait_ge(weights_loaded, 6 * DMA)
            pe.wait_ge(silu_done, 1)
            for k in range(3):
                for c in range(EC):
                    last = nc.tensor.matmul(ps[0:B, k, :], silu[:, c, :], wmod_sb[:, c, k * 512:(k + 1) * 512], start=(c == 0), stop=(c == EC - 1))
            last.then_inc(mod_product, 1)
            pe.wait_ge(w_sum_done, 1)
            pe.wait_ge(consts_set, 8)
            nc.tensor.matmul(ps[:, 3, 0:1], ones[:, :], w_sum[:, :], start=True, stop=True).then_inc(w_total, 1)
            pe.wait_ge(ident_set, 2)
            pe.wait_ge(setup_done, 1)

            def transposes(src, c):
                for n in range(BPC):
                    last = nc.tensor.transpose(aux[:, n * P:(n + 1) * P], src[:, n, c * P:(c + 1) * P], ident[:, :])
                return last

            def token_products(hT, w, n0):
                for n in range(n0, n0 + 2):
                    for c in range(EC):
                        last = nc.tensor.matmul(aux[:, (n - n0) * E:(n - n0 + 1) * E], hT[:, c, n * P:(n + 1) * P], w[:, c, :],
                                                start=(c == 0), stop=(c == EC - 1))
                return last

            def a_step(job, i):
                if i == 0:
                    pe.wait_ge(a_normed, job + 1)
                else:
                    pe.wait_ge(a_evacuated, job * A_STEPS + i)
                if i < 2:
                    last = transposes(normed, i)
                elif i < 6:
                    w = (wq, wk)[(i - 2) // 2]
                    f = (i - 2) % 2
                    for c in range(EC):
                        last = nc.tensor.matmul(aux, w[:, c, f * P:(f + 1) * P], a_hT[:, c, :], start=(c == 0), stop=(c == EC - 1))
                else:
                    last = token_products(a_hT, wv, (i - 6) * 2)
                last.then_inc(a_product, 1)

            def e_step(job, i):
                if i == 0:
                    pe.wait_ge(e_loaded, (job + 1) * 7 * DMA)
                    pe.wait_ge(e_open, job + 1)
                else:
                    pe.wait_ge(e_evacuated, job * E_STEPS + i)
                if i < 2:
                    last = token_products(e_attn, wo, i * 2)
                elif i < 4:
                    pe.wait_ge(e_normed, job + 1)
                    last = transposes(normed, i - 2)
                else:
                    last = token_products(e_hT, wf, (i - 4) * 2)
                last.then_inc(e_product, 1)

            def scores(body, u, n):
                buf, tc, blk = u // UNITS, u // NB % NC, u % NB
                if n >= SLOTS:
                    pe.wait_ge(exp_done, body * (2 * BODY) + n - SLOTS + 1)
                for half in range(2):
                    at = 64 * half
                    last = nc.tensor.matmul(slots[n % SLOTS][:, half, :], keys[buf][at:at + KS_ROWS, n % PAIRS, blk * P:(blk + 1) * P],
                                            queries[buf][at:at + KS_ROWS, n % PAIRS, tc * CH:(tc + 1) * CH], start=True, stop=True)
                last.then_inc(scores_ready, 1)

            def weighted(body, u):
                buf, blk, seg = u // UNITS, u % NB, u // NB
                if blk == 0:
                    pe.wait_ge(pv_read, body * SEGS + seg + 1)
                pe.wait_ge(exp_done, body * (2 * BODY) + PAIRS * (u + 1))
                for pair in range(PAIRS):
                    for half in range(2):
                        j = 32 * (2 * pair + half)
                        last = nc.tensor.matmul(pv[j:j + VW, :], values[buf][:, blk, half, :], probs[:, u % PRING, pair, half, :],
                                                start=(blk == 0), stop=(blk == NB - 1))
                last.then_inc(pv_done, 1)

            with pe.Fori(0, NC) as tc:
                for i in range(A_STEPS):
                    a_step(tc, i)

            exact_runs = pe.alloc_register("pe_exact_runs")
            pe.reg_mov(exact_runs, 0)
            with pe.Fori(0, B) as b:
                wait_alone(pe, m_open, b + 1, pe_passed)
                for blk in range(NB):
                    for c in range(EC):
                        at = (blk % 2) * (NS * BOX) + c * (NS // EC) * BOX
                        for sign in range(2):
                            last = nc.tensor.matmul(ps[:, blk // 2, at:at + (NS // EC) * BOX], q_sign[:, c, sign, blk * P:(blk + 1) * P],
                                                    box_w[:, c, sign, :, :].rearrange("p h k -> p (h k)"), start=(sign == 0), stop=(sign == 1))
                last.then_inc(m_bounds, 1)
                pe.wait_ge(m_crit_done, b + 1)
                nc.tensor.transpose(ps[0:1, 0, 0:P], m_crit[:, 0:1], ident[:, :]).then_inc(m_crit_row, 1)
                wait_alone(pe, m_flag_set, b + 1, pe_passed)
                exact = pe.value_load(m_flag[0:1, 0:1], min_val=0, max_val=1)
                with pe.If(exact > 0):
                    runs = pe.snap(exact_runs, min_val=0, max_val=B - 1)
                    with pe.Fori(0, NG) as g:
                        pe.wait_ge(m_rows_loaded, (runs * (NG + 1) + g + 1) * (ROW_LOADS * DMA))
                        for n in range(4 * NB):
                            head, blk = n // NB, n % NB
                            pair, at = head // 2, 64 * (head % 2)
                            pe.wait_ge(m_reduced, (runs * NG + g) * (4 * NB) + n + 1)
                            for k in range(NC):
                                last = nc.tensor.matmul(ps[:, 4 * (n % 2) + k, :], queries[0][at:at + KQ, pair, blk * P:(blk + 1) * P],
                                                        keys[0][at:at + KQ, pair, k * CH:(k + 1) * CH], start=True, stop=True)
                            last.then_inc(m_scores, 1)
                    wait_alone(pe, m_reduced, (runs + 1) * NG * (4 * NB) + 2, pe_passed)
                    pe.reg_add(exact_runs, exact_runs, 1)
                for blk in range(NB):
                    last = nc.tensor.transpose(ps[0:NS, blk // BPC, (blk % BPC) * P:(blk % BPC + 1) * P], m_cols[:, blk, :], ident[:, :])
                last.then_inc(m_transposed, 1)
                wait_alone(pe, m_done, b + 1, pe_passed)

                with pe.Fori(0, GP) as gp:
                    body = b * GP + gp
                    ejob = (body + (B - 1) * GP) % (B * GP)
                    for u in range(BODY + LAG):
                        if u < BODY:
                            if u % UNITS == 0:
                                buf = u // UNITS
                                pe.wait_ge(group_loaded[buf], (body + 1) * (GROUP_LOADS * DMA))
                            for n in (PAIRS * u, PAIRS * u + 1):
                                scores(body, u, n)
                        if u >= LAG:
                            weighted(body, u - LAG)
                        if u in STEP_UNITS:
                            i = STEP_UNITS.index(u)
                            if i < A_STEPS:
                                with pe.If(b < B - 1):
                                    a_step(body + NC, i)
                            elif i < A_STEPS + E_STEPS:
                                with pe.If(b > 0):
                                    e_step(ejob, i - A_STEPS)

            with pe.Fori(0, NC) as tc:
                for i in range(E_STEPS):
                    e_step((B - 1) * NC + tc, i)

        @block.vector
        def _(dve):
            V = nc.vector
            link = Chain(dve, start_chain, 0)
            dve.wait_ge(c_exp_done, 1)
            link.then(V.tensor_scalar(c_exp[:, :, :], c_exp[:, :, :], 1.0, None, ALU.add))
            link.then(V.reciprocal(c_exp[:, :, :], c_exp[:, :, :]))
            V.tensor_tensor(silu[:, :, :], c_sb[:, :, :], c_exp[:, :, :], ALU.mult).then_inc(silu_done, 1)
            lam4 = lam_in[:, :, :].rearrange("p (i j) d -> p i j d", j=2)
            link.then(V.tensor_tensor(lam_prod[:, :, :], lam4[:, :, 0, :], lam4[:, :, 1, :], ALU.mult))
            V.tensor_reduce(lam_sum[:, :], lam_prod[:, :, :], axis=AX.X, op=ALU.add).then_inc(lam_sum_done, 1)
            dve.wait_ge(weights_loaded, 6 * DMA)
            V.tensor_reduce(w_sum[:, :], wf[:, :, :], axis=AX.XY, op=ALU.add, apply_absolute_value=True).then_inc(w_sum_done, 1)
            dve.wait_ge(lam_exp_done, 1)
            link.then(V.tensor_scalar(coef[:, :], lam_exp[:, 1:2], lam_exp[:, 0:1], -LAMBDA_INIT, ALU.subtract, ALU.add))
            link.then(V.memset(coef[0:64, :], 1.0))
            dve.wait_ge(mod_product, 1)
            link.then(V.tensor_copy(mod_sb[:, :, :].rearrange("b k e -> b (k e)"), ps[0:B, 0:3, :].rearrange("b k e -> b (k e)")))
            for kind in (1, 4):
                V.tensor_scalar(mod_sb[:, kind, :], mod_sb[:, kind, :], 1.0, None, ALU.add)
            for kind in (2, 5):
                link.then(V.scalar_tensor_tensor(gate_abs[:, :], mod_sb[:, kind, :], -1.0, mod_sb[:, kind, :], ALU.mult, ALU.max))
                V.tensor_scalar(gate_abs[:, :], gate_abs[:, :], 0.25, None, ALU.max)
                link.then(V.tensor_scalar(gate_sign[:, :], mod_sb[:, kind, :], 0.0, 2.0, ALU.is_ge, ALU.mult))
                link.then(V.scalar_tensor_tensor(mod_sb[:, kind, :], gate_sign[:, :], -1.0, gate_abs[:, :], ALU.add, ALU.mult))
            V.tensor_copy(e_open_t[0:B, :], mod_sb[:, 0, 0:1]).then_inc(mod_done, 1)
            dve.wait_ge(w_total, 1)
            link.then(V.tensor_scalar(w_scale[:, :], ps[:, 3, 0:1], 1.0 / (E * E), 1e-5, ALU.mult, ALU.max))
            V.tensor_scalar(w_half[:, 0:1], w_scale[:, :], 0.5, None, ALU.mult)
            link.then(V.tensor_scalar(w_half[:, 1:2], w_scale[:, :], -0.5, None, ALU.mult))
            V.tensor_scalar(w_low[:, :, :], wf[:, :, :], w_half[:, 1:2], w_scale[:, :], ALU.is_lt, ALU.mult)
            link.then(V.tensor_scalar(wf[:, :, :], wf[:, :, :], w_half[:, 0:1], w_scale[:, :], ALU.is_gt, ALU.mult))
            link.then(V.tensor_tensor(wf[:, :, :], wf[:, :, :], w_low[:, :, :], ALU.subtract))
            V.memset(e_open_t[:, :], 0.0).then_inc(pv_read, 1)
            link.then(V.memset(seg_r[:, :], 0.0))
            V.memset(seg_rc[:, :], 0.0).then_inc(m_reduced, 2)
            V.memset(stats[:, 0, :], 0.0).then_inc(setup_done, 1)
            dve.wait_ge(setup_done, 1)

            def norm(link, src, ve, rstd, var_sem, rstd_sem, job, done):
                for n in range(BPC):
                    last = V.bn_stats(stats[:, n, :], src[:, n, :])
                link.then(last)
                dve.sem_inc(dve_passed, 1)
                for n in range(BPC):
                    last = V.bn_aggr(moments[:, n, :], stats[:, n, :])
                link.then(last)
                V.tensor_scalar(ve[:, :], moments[:, :, 1], EPS, None, ALU.add).then_inc(var_sem, 1)
                dve.wait_ge(rstd_sem, job + 1)
                for n in range(BPC):
                    last = V.tensor_scalar(normed[:, n, :], src[:, n, :], moments[:, n, 0:1], rstd[:, n:n + 1], ALU.subtract, ALU.mult)
                last.then_inc(done, 1)

            def a_norm(job):
                dve.wait_ge(a_loaded, (job + 1) * 3 * DMA)
                norm(Chain(dve, a_chain, job * 2), a_x, a_ve, a_rstd, a_var, a_rstd_done, job, a_normed)

            def a_bounds(job, i, tc):
                c = i % 2
                wait_alone(dve, a_evacuated, job * A_STEPS + 3 + i, dve_passed)
                src, at = a_qk[:, i, :], bass.ds(tc, 1)
                if i < 2:
                    for sign, op in enumerate((ALU.max, ALU.min)):
                        V.tensor_scalar(q_sign[:, c, sign, bass.ds(tc * CH, CH)], src, 0.0, None, op)
                    last = V.tensor_reduce(a_qabs[:, c, at], src, axis=AX.X, op=ALU.max, apply_absolute_value=True)
                else:
                    V.tensor_reduce(box[:, c, 0, at], src, axis=AX.X, op=ALU.max)
                    V.tensor_reduce(box[:, c, 1, at], src, axis=AX.X, op=ALU.min)
                    last = V.tensor_reduce(a_sum[:, c, at], src, axis=AX.X, op=ALU.add)
                last.then_inc(a_bounded, 1)
                wait_alone(dve, a_bounded, job * 4 + i + 1, dve_passed)

            def a_evacuate(job, i, tc):
                dve.wait_ge(a_product, job * A_STEPS + i + 1)
                if i < 2:
                    last = V.tensor_scalar(a_hT[:, i, :], aux, a_cols[:, 1, i:i + 1], a_cols[:, 0, i:i + 1], ALU.mult, ALU.add)
                elif i < 6:
                    last = V.tensor_scalar(a_qk[:, i - 2, :], aux, SCALING if i < 4 else 1.0, None, ALU.mult)
                else:
                    for n in range(2):
                        last = V.tensor_copy(a_v[:, :, (i - 6) * 2 + n, :, 0:VD], aux[:, n * E:(n + 1) * E].rearrange("p (g h d) -> p g h d", g=NG, h=2))
                last.then_inc(a_evacuated, 1)
                if 2 <= i < 6:
                    a_bounds(job, i - 2, tc)

            def e_evacuate(job, i):
                if i == 0:
                    dve.wait_ge(e_loaded, (job + 1) * 7 * DMA)
                    V.tensor_copy(e_open_t[:, :], e_cols[:, 0, 0:1]).then_inc(e_open, 1)
                link = Chain(dve, e_chain, job * E_LINKS + (0, 1, 4, 4, 4, 5)[i])
                dve.wait_ge(e_product, job * E_STEPS + i + 1)
                two = aux.rearrange("p (n e) -> p n e", n=2)
                n0 = (i % 2) * 2
                if i in (2, 3):
                    V.tensor_scalar(e_hT[:, i - 2, :], aux, e_cols[:, 1, i - 2:i - 1], e_cols[:, 0, i - 2:i - 1], ALU.mult, ALU.add).then_inc(e_evacuated, 1)
                    return
                gate, base, dst = (0, e_x, e_x2) if i < 2 else (1, e_x2, e_y)
                link.then(V.tensor_tensor(e_tmp[:, :, :], two, e_gate[:, gate:gate + 1, :].broadcast_to([P, 2, E]), ALU.mult))
                V.tensor_tensor(dst[:, n0:n0 + 2, :], e_tmp[:, :, :], base[:, n0:n0 + 2, :], ALU.add).then_inc(e_evacuated, 1)
                wait_alone(dve, e_evacuated, job * E_STEPS + i + 1, dve_passed)
                if i == 1:
                    norm(link, e_x2, e_ve, e_rstd, e_var, e_rstd_done, job, e_normed)

            def segment(body, s):
                NQ = CH // 32
                link = Chain(dve, s_chain, (body * SEGS + s) * S_LINKS)
                if s:
                    wait_alone(dve, seg_stored, (body * SEGS + s) * DMA, dve_passed)
                else:
                    with dve.If(body > 0):
                        wait_alone(dve, seg_stored, body * (SEGS * DMA), dve_passed)
                dve.wait_ge(pv_done, body * BODY + (s + 1) * NB)
                V.transpose(seg_t[:, :, :].rearrange("p c d -> p (c d)"), pv).then_inc(pv_read, 1)
                dve.wait_ge(pv_read, body * SEGS + s + 2)
                link.then(V.reciprocal(seg_r[:, :], seg_t[:, :, VD]))
                link.then(V.tensor_scalar(seg_rc[:, :], seg_r[:, :], coef[:, 0:1], None, ALU.mult))
                link.then(V.tensor_tensor(seg_w[:, :, :], seg_t[:, :, 0:VD], seg_rc[:, :].rearrange("p (c o) -> p c o", o=1).broadcast_to([P, NQ, VD]), ALU.mult))
                link.then(V.tensor_copy(seg_w2[:, :, :], seg_w[64:128, :, :]))
                link.then(V.tensor_tensor(seg_d[:, :, :], seg_w[0:64, :, :], seg_w2[:, :, :], ALU.add))
                link.then(V.tensor_tensor(seg_sq[:, :, :], seg_d[:, :, :], seg_d[:, :, :], ALU.mult))
                link.then(V.tensor_reduce(seg_ss[0:64, :], seg_sq[:, :, :], axis=AX.X, op=ALU.add))
                V.tensor_scalar(seg_ms[:, :], seg_ss[0:64, :], 1.0 / VD, EPS, ALU.mult, ALU.add).then_inc(seg_ms_done, 1)
                dve.wait_ge(seg_rs_done, body * SEGS + s + 1)
                V.tensor_tensor(seg_n[:, :, :], seg_d[:, :, :], seg_rs[:, :].rearrange("p (c o) -> p c o", o=1).broadcast_to([64, NQ, VD]), ALU.mult).then_inc(s_chain_n, 1)
                dve.wait_ge(s_chain_n, (body * SEGS + s) * 2 + 1)
                for h in range(2):
                    q = slice(32 * h, 32 * h + 32)
                    last = V.scalar_tensor_tensor(seg_a[:, :, h * VD:(h + 1) * VD], seg_n[q, :, :], 1.0 - LAMBDA_INIT,
                                                  subln_sb[q, :].rearrange("p (o d) -> p o d", o=1).broadcast_to([32, NQ, VD]), ALU.mult, ALU.mult)
                last.then_inc(s_chain_n, 1)
                dve.wait_ge(s_chain_n, (body * SEGS + s) * 2 + 2)
                V.transpose(seg_o[:, :], seg_a[:, :, :].rearrange("p c d -> p (c d)")).then_inc(seg_done, 1)

            with dve.Fori(0, NC) as tc:
                a_norm(tc)
                for i in range(A_STEPS):
                    a_evacuate(tc, i, tc)

            exact_runs = dve.alloc_register("dve_exact_runs")
            dve.reg_mov(exact_runs, 0)
            with dve.Fori(0, B) as b:
                HH = NS // EC
                link = Chain(dve, m_chain, b * M_LINKS)
                link.then(V.tensor_reduce(m_mean[:, :], a_sum[:, :, :], axis=AX.X, op=ALU.add))
                for sign in range(2):
                    last = V.tensor_scalar(box[:, :, sign, NC], m_mean[:, :], 1.0 / T, None, ALU.mult)
                link.then(last)
                for c in range(EC):
                    for sign in range(2):
                        last = V.tensor_tensor(box_w[:, c, sign, :, :], head_mask[:, :].rearrange("p (h o) -> p h o", o=1).broadcast_to([P, HH, BOX]),
                                               box[:, c, sign:sign + 1, :].broadcast_to([P, HH, BOX]), ALU.mult)
                last.then_inc(m_open, 1)
                for sign in range(2):
                    V.tensor_reduce(m_size[:, sign, :], box[:, :, sign, 0:NC], axis=AX.X, op=ALU.max, apply_absolute_value=True)
                link.then(V.tensor_reduce(m_size[:, 2, :], a_qabs[:, :, :], axis=AX.X, op=ALU.max))
                link.then(V.tensor_tensor(m_size[:, 3, :], m_size[:, 0, :], m_size[:, 1, :], ALU.max))
                link.then(V.scalar_tensor_tensor(m_size[:, 0, :], m_size[:, 3, :], MAX_SLACK / MAX_SIZE, m_size[:, 2, :], ALU.mult, ALU.mult))
                link.then(V.tensor_reduce(m_crit[:, 1:2], m_size[:, 0, :], axis=AX.X, op=ALU.max))
                wait_alone(dve, m_bounds, b + 1, dve_passed)
                bound = ps[:, :, 0:2 * NS * BOX].rearrange("p a (h k) -> p a h k", k=BOX)
                cols = m_cols[:, :, :].rearrange("p (a i) h -> p a (i h)", i=2)
                link.then(V.tensor_reduce(cols, bound[:, :, :, 0:NC], axis=AX.X, op=ALU.max))
                link.then(V.tensor_tensor(m_slack[:, :].rearrange("p (a h) -> p a h", a=8), cols, bound[:, :, :, NC], ALU.subtract))
                link.then(V.tensor_reduce(m_crit[:, 2:3], m_slack[:, :], axis=AX.X, op=ALU.max))
                V.tensor_tensor(m_crit[:, 0:1], m_crit[:, 1:2], m_crit[:, 2:3], ALU.max).then_inc(m_crit_done, 1)
                dve.wait_ge(m_crit_row, b + 1)
                link.then(V.tensor_reduce(m_worst[:, :], ps[0:1, 0, 0:P], axis=AX.X, op=ALU.max))
                V.tensor_scalar(m_flag[:, :], m_worst[:, :], MAX_SLACK, None, ALU.is_gt).then_inc(m_flag_set, 1)
                wait_alone(dve, m_flag_set, b + 1, dve_passed)
                exact = dve.value_load(m_flag[0:1, 0:1], min_val=0, max_val=1)
                with dve.If(exact > 0):
                    runs = dve.snap(exact_runs, min_val=0, max_val=B - 1)
                    with dve.Fori(0, NG) as g:
                        for n in range(4 * NB):
                            head, blk = n // NB, n % NB
                            shead = 2 * (head % 2) + head // 2
                            wait_alone(dve, m_scores, (runs * NG + g) * (4 * NB) + n + 1, dve_passed)
                            V.tensor_reduce(m_cols[:, blk, bass.ds(g * 4 + shead, 1)], ps[:, 4 * (n % 2):4 * (n % 2) + 4, :], axis=AX.XY, op=ALU.max).then_inc(m_reduced, 1)
                    dve.reg_add(exact_runs, exact_runs, 1)
                dve.wait_ge(m_transposed, b + 1)
                link.then(V.tensor_scalar(m_rows, ps[0:NS, 0:4, :].rearrange("p a b -> p (a b)"), -1.0, HEADROOM, ALU.mult, ALU.add))
                link.then(V.tensor_copy(m_parts[:, 0, :], m_rows))
                link.then(V.tensor_tensor(m_rows, m_rows, m_parts[:, 0, :], ALU.subtract))
                link.then(V.tensor_copy(m_parts[:, 1, :], m_rows))
                V.tensor_tensor(m_parts[:, 2, :], m_rows, m_parts[:, 1, :], ALU.subtract).then_inc(m_done, 1)

                with dve.Fori(0, GP) as gp:
                    body = b * GP + gp
                    ejob = (body + (B - 1) * GP) % (B * GP)
                    with dve.If(b < B - 1):
                        a_norm(body + NC)
                    for s in range(SEGS):
                        for i in (2 * s, 2 * s + 1):
                            if i < A_STEPS:
                                with dve.If(b < B - 1):
                                    a_evacuate(body + NC, i, gp)
                            elif i < A_STEPS + E_STEPS:
                                with dve.If(b > 0):
                                    e_evacuate(ejob, i - A_STEPS)
                        segment(body, s)

            with dve.Fori(0, NC) as tc:
                for i in range(E_STEPS):
                    e_evacuate((B - 1) * NC + tc, i)


_OUTS = [((4, 2048, 256), "float32")]


def kernel(**inputs):
    import concourse.bacc as _bacc
    from concourse.bass_utils import run_bass_kernel_spmd as _run

    nc = _bacc.Bacc("TRN2", target_bir_lowering=False, num_devices=1)
    plain = {k: np.asarray(v) for k, v in inputs.items()}
    laid = [
        ("x", plain["L0_attn_query"]),
        ("wqT", plain["L0_attn_Wq"].T), ("wkT", plain["L0_attn_Wk"].T), ("wvT", plain["L0_attn_Wv"].T), ("woT", plain["L0_attn_Wo"].T),
        ("lq1", plain["L0_attn_lambda_q1"]), ("lk1", plain["L0_attn_lambda_k1"]),
        ("lq2", plain["L0_attn_lambda_q2"]), ("lk2", plain["L0_attn_lambda_k2"]),
        ("subln", plain["L0_attn_subln_w"]), ("wfT", plain["L0_ffn_weight"].T),
        ("cT", plain["L0_c"].T), ("wmod", plain["L0_wmod"]),
    ]
    arrays, args = {}, []
    for name, a in laid:
        a = np.ascontiguousarray(a)
        arrays[f"in_{name}_dram"] = a
        args.append(nc.dram_tensor(f"in_{name}_dram", a.shape, mybir.dt.from_np(a.dtype), kind="ExternalInput").ap())
    for i, (shape, dtype) in enumerate(_OUTS):
        args.append(nc.dram_tensor(f"out_{i}_dram", shape, mybir.dt.from_np(np.dtype(dtype)), kind="ExternalOutput").ap())
    adaln_diff_attention(nc, *args)
    r = _run(nc, [arrays], core_ids=[0])
    return r.results[0]["out_0_dram"]
```

```python
from contextlib import ExitStack

import numpy as np

import concourse.bass as bass
from concourse import mybir

ALU = mybir.AluOpType
ACT = mybir.ActivationFunctionType
AX = mybir.AxisListType
F32 = mybir.dt.float32
BF16 = mybir.dt.bfloat16
P = 128


def wait_alone(eng, sem, value, passed):
    eng.wait_ge(sem, value)
    eng.sem_inc(passed, 1)


class Chain:

    def __init__(self, eng, sem, start, passed=None):
        self.eng, self.sem, self.start, self.count, self.passed = eng, sem, start, 0, passed

    def then(self, instruction):
        self.count += 1
        instruction.then_inc(self.sem, 1)
        self.eng.wait_ge(self.sem, self.start + self.count)
        if self.passed:
            self.eng.sem_inc(self.passed, 1)


def adaln_diff_attention(nc, x, wqT, wkT, wvT, woT, lq1, lk1, lq2, lk2, subln, wfT, cT, wmod, out):
    B, T, E = x.shape
    HD = lq1.shape[0]
    VD = 2 * HD
    NH = E // VD
    NS = 2 * NH
    NG = NS // 4
    CH = 512
    NC = T // CH
    NB = T // P
    BPC = CH // P
    EC = E // P
    PAIRS = 2
    SLOTS = 3
    PRING = 4
    LAG = 2
    VW = 32
    PARTS = 3
    UNITS = NC * NB
    BODY = 2 * UNITS
    SEGS = 2 * NC
    GP = NG // 2
    assert GP == NC
    QK_ROWS = [(0, 0), (0, 1), (1, 0), (1, 1), (0, 2), (2, 0)]
    KQ = HD * len(QK_ROWS)
    KS_ROWS = 64
    BOX = NC + 1
    HEADROOM = 20.0
    MAX_SLACK = 80.0
    MAX_SIZE = 256.0
    LAMBDA_INIT = float(0.8 - 0.6 * np.exp(-0.3 * 12))
    SCALING = float(np.float32(HD ** -0.5))
    EPS = 1e-5
    A_STEPS, E_STEPS = 8, 6
    STEP_UNITS = [NB * (n // 2) + (9, 13)[n % 2] for n in range(A_STEPS + E_STEPS)]
    M_STEPS = 8 + 1 + NC
    M_GROUPS = {3: [0, 1, 2], 4: [3, 4, 5], 5: [6, 7, 8], 6: [9, 10]}
    M_UNITS = {NB * s + 10 + (2 * k if s == 6 else k): i for s, steps in M_GROUPS.items() for k, i in enumerate(steps)}
    M_UNITS |= {NB * 6 + 15: 11, NB * 7 + 9: 12}
    S_LINKS, E_LINKS, P_LINKS = 7, 6, 4
    LAST_E = [(0, 0), (0, 1)]
    for j in range(NC):
        LAST_E += [(j, 2), (j, 3)] + ([(j + 1, 0), (j + 1, 1)] if j < NC - 1 else []) + [(j, 4), (j, 5)]
    LAST_JOB = (B - 1) * NC
    M_LINKS = 2 + 4 + 8 + 1 + P_LINKS * NC
    GROUP_LOADS = 2 * 2 * len(QK_ROWS) + 2 + 1
    ROW_LOADS = 2 * 2 * len(QK_ROWS)
    EXACT_LOADS = (NG + 1) * ROW_LOADS + 1 + 2
    A_STORES = 4 + NG
    DMA = 16

    q_scr = nc.dram_tensor("q_scr", [B, PARTS, E, T], BF16, kind="Internal").ap()
    k_scr = nc.dram_tensor("k_scr", [B, PARTS, E, T], BF16, kind="Internal").ap()
    v_scr = nc.dram_tensor("v_scr", [B, NG, P, NB, 2 * VW], F32, kind="Internal").ap()
    m_scr = nc.dram_tensor("m_scr", [B, PARTS, NS, T], BF16, kind="Internal").ap()
    attn_scr = nc.dram_tensor("attn_scr", [B, E, T], F32, kind="Internal").ap()
    mod_scr = nc.dram_tensor("mod_scr", [B, 6, E], F32, kind="Internal").ap()

    with ExitStack() as ctx:
        def sb(name, shape, dt=F32):
            return ctx.enter_context(nc.sbuf_tensor(name, shape, dt))

        def sem(name):
            return ctx.enter_context(nc.semaphore(name))

        ident = sb("ident", [P, P])
        ones = sb("ones", [P, P])
        neg_half = sb("neg_half", [P, 16])
        wq, wk, wv, wo, wf = (sb(f"w_{n}", [P, EC, E]) for n in ("q", "k", "v", "o", "f"))
        wmod_sb = sb("wmod_sb", [P, EC, 6 * E])
        c_sb = sb("c_sb", [P, EC, B])
        c_exp = sb("c_exp", [P, EC, B])
        silu = sb("silu", [P, EC, B])
        mod_sb = sb("mod_sb", [B, 6, E])
        gate_abs = sb("gate_abs", [B, E])
        gate_sign = sb("gate_sign", [B, E])
        w_sum = sb("w_sum", [P, 1])
        w_scale = sb("w_scale", [P, 1])
        w_half = sb("w_half", [P, 2])
        w_low = sb("w_low", [P, EC, E])
        lam_in = sb("lam_in", [P, 4, HD])
        lam_prod = sb("lam_prod", [P, 2, HD])
        lam_sum = sb("lam_sum", [P, 2])
        lam_exp = sb("lam_exp", [P, 2])
        act_open = sb("act_open", [P, 2])
        coef = sb("coef", [P, 1])
        subln_sb = sb("subln_sb", [2 * 32, VD])
        keys = [sb(f"keys{i}", [P, PAIRS, T], BF16) for i in range(2)]
        queries = [sb(f"queries{i}", [P, PAIRS, T], BF16) for i in range(2)]
        values = [sb(f"values{i}", [P, NB, 2, VW]) for i in range(2)]
        probs = sb("probs", [P, PRING, PAIRS, 2, CH])
        seg_t = sb("seg_t", [P, CH // 32, 32])
        seg_r = sb("seg_r", [P, CH // 32])
        seg_rc = sb("seg_rc", [P, CH // 32])
        seg_w = sb("seg_w", [P, CH // 32, VD])
        seg_w2 = sb("seg_w2", [64, CH // 32, VD])
        seg_d = sb("seg_d", [64, CH // 32, VD])
        seg_sq = sb("seg_sq", [64, CH // 32, VD])
        seg_ss = sb("seg_ss", [64, CH // 32])
        seg_ms = sb("seg_ms", [64, CH // 32])
        seg_rs = sb("seg_rs", [64, CH // 32])
        seg_n = sb("seg_n", [64, CH // 32, VD])
        seg_a = sb("seg_a", [32, CH // 32, 2 * VD])
        seg_o = sb("seg_o", [32, CH])
        a_x = sb("a_x", [P, BPC, E])
        a_cols = sb("a_cols", [P, 2, EC])
        stats = sb("stats", [P, BPC, 6])
        moments = sb("moments", [P, BPC, 2])
        a_ve = sb("a_ve", [P, BPC])
        a_rstd = sb("a_rstd", [P, BPC])
        normed = sb("normed", [P, BPC, E])
        a_hT = sb("a_hT", [P, EC, CH])
        a_qk = sb("a_qk", [P, 4, CH])
        a_rest = sb("a_rest", [P, CH])
        a_sum = sb("a_sum", [P, EC, NC])
        a_qabs = sb("a_qabs", [P, EC, NC])
        box = sb("box", [P, EC, 2, BOX])
        q_sign = sb("q_sign", [P, EC, 2, T], BF16)
        a_parts = sb("a_parts", [P, 4, PARTS, CH], BF16)
        a_v = sb("a_v", [P, NG, BPC, 2, VW])
        e_attn = sb("e_attn", [P, EC, CH])
        e_x = sb("e_x", [P, BPC, E])
        e_cols = sb("e_cols", [P, 2, EC])
        e_gate = sb("e_gate", [P, 2, E])
        e_open_t = sb("e_open_t", [P, 1])
        e_tmp = sb("e_tmp", [P, 2, E])
        e_x2 = sb("e_x2", [P, BPC, E])
        e_ve = sb("e_ve", [P, BPC])
        e_rstd = sb("e_rstd", [P, BPC])
        e_hT = sb("e_hT", [P, EC, CH])
        e_y = sb("e_y", [P, BPC, E])
        head_mask = sb("head_mask", [P, NS // EC])
        box_w = sb("box_w", [P, EC, 2, NS // EC, BOX], BF16)
        m_mean = sb("m_mean", [P, EC])
        m_size = sb("m_size", [P, 4, EC])
        m_slack = sb("m_slack", [P, NB * NS])
        m_crit = sb("m_crit", [P, 3])
        m_worst = sb("m_worst", [1, 1])
        m_flag = sb("m_flag", [1, 1], mybir.dt.int32)
        m_cols = sb("m_cols", [P, NB, NS])
        m_rows = w_low[0:NS, :, :].rearrange("p c f -> p (c f)")
        m_parts = wmod_sb[0:NS, :, :].rearrange("p c f -> p (c f)").bitcast(BF16).rearrange("p (i t) -> p i t", i=PARTS)

        ps = ctx.enter_context(nc.psum_tensor("ps", [P, 8, 512], F32))
        slots = [ps[:, 2 * s:2 * s + 2, :] for s in range(SLOTS)]
        pv = ps[:, 6, :]

        def slot_of(n):
            assert 2 * BODY % SLOTS == 1
            return n % SLOTS if n < 2 * BODY - 1 else 1

        aux = ps[:, 7, :]

        sp_passed, pool_passed, pe_passed, dve_passed = (sem(f"{e}_passed") for e in ("sp", "pool", "pe", "dve"))
        consts_set = sem("consts_set")
        ident_set = sem("ident_set")
        weights_loaded = sem("weights_loaded")
        wmod_loaded = sem("wmod_loaded")
        small_loaded = sem("small_loaded")
        c_exp_done = sem("c_exp_done")
        start_chain = sem("start_chain")
        silu_done = sem("silu_done")
        mod_product = sem("mod_product")
        mod_done = sem("mod_done")
        mod_stored = sem("mod_stored")
        w_sum_done = sem("w_sum_done")
        w_total = sem("w_total")
        setup_done = sem("setup_done")
        lam_sum_done = sem("lam_sum_done")
        lam_exp_done = sem("lam_exp_done")
        a_loaded = sem("a_loaded")
        a_var = sem("a_var")
        a_rstd_done = sem("a_rstd_done")
        a_normed = sem("a_normed")
        a_product = sem("a_product")
        a_evacuated = sem("a_evacuated")
        a_bounded = sem("a_bounded")
        a_split = sem("a_split")
        a_pool_chain = sem("a_pool_chain")
        a_chain = sem("a_chain")
        a_stored = sem("a_stored")
        a_cols_loaded = sem("a_cols_loaded")
        a_head = sem("a_head")
        a_rest_done = sem("a_rest_done")
        a_middle = sem("a_middle")
        e_loaded = sem("e_loaded")
        e_mod_loaded = sem("e_mod_loaded")
        e_open = sem("e_open")
        e_product = sem("e_product")
        e_evacuated = sem("e_evacuated")
        e_var = sem("e_var")
        e_rstd_done = sem("e_rstd_done")
        e_normed = sem("e_normed")
        e_chain = sem("e_chain")
        e_stored = sem("e_stored")
        m_open = sem("m_open")
        m_rows_loaded = sem("m_rows_loaded")
        m_scores = sem("m_scores")
        m_reduced = sem("m_reduced")
        m_product = sem("m_product")
        m_evacuated = sem("m_evacuated")
        m_crit_done = sem("m_crit_done")
        m_flag_set = sem("m_flag_set")
        m_chain = sem("m_chain")
        m_done = sem("m_done")
        exact_product = sem("exact_product")
        exact_evacuated = sem("exact_evacuated")
        exact_chain = sem("exact_chain")
        exact_done = sem("exact_done")
        m_stored = sem("m_stored")
        group_loaded = [sem(f"group_loaded{i}") for i in range(2)]
        scores_ready = sem("scores_ready")
        exp_done = sem("exp_done")
        pv_done = sem("pv_done")
        pv_read = sem("pv_read")
        s_chain = sem("s_chain")
        s_chain_n = sem("s_chain_n")
        seg_ms_done = sem("seg_ms_done")
        seg_rs_done = sem("seg_rs_done")
        seg_done = sem("seg_done")
        seg_stored = sem("seg_stored")

        block = ctx.enter_context(nc.Block())

        @block.sync
        def _(sp):
            def inside(value, most, why):
                return nc.s_assert_within(value, 0, most, skip_runtime_bounds_check_because=why)

            def a_load(b, tc):
                sp.dma_start(a_x[:, :, :], x[bass.ds(b, 1), bass.ds(tc * CH, CH), :].rearrange("o (n p) e -> p (o n) e", p=P)).then_inc(a_loaded, DMA)

            def a_columns(b):
                for c in range(EC):
                    sp.dma_start(a_cols[:, :, c], mod_scr[bass.ds(b, 1), 0:2, c * P:(c + 1) * P].rearrange("o k p -> p (o k)"), allow_slow_non_contiguous=True).then_inc(a_cols_loaded, DMA)

            def a_store_qk(job, b, tc, i):
                wait_alone(sp, a_split, (job + 1) * 4 + i + 1, sp_passed)
                dst = (q_scr, k_scr)[i // 2]
                c = i % 2
                sp.dma_start(dst[bass.ds(b, 1), :, c * P:(c + 1) * P, bass.ds(tc * CH, CH)].rearrange("o s p t -> p (o s) t"),
                             a_parts[:, i, :, :]).then_inc(a_stored, DMA)

            def a_store_v(job, b, tc):
                sp.wait_ge(a_evacuated, (job + 1) * A_STEPS)
                for g in range(NG):
                    sp.dma_start(v_scr[bass.ds(b, 1), g, :, bass.ds(tc * BPC, BPC), :].rearrange("o p n w -> p (o n) w"),
                                 a_v[:, g, :, :, :].rearrange("p n h w -> p n (h w)")).then_inc(a_stored, DMA)

            def a_wait(jobs):
                wait_alone(sp, a_stored, (jobs + 1) * A_STORES * DMA, sp_passed)

            def e_loads(b, tc):
                for c in range(EC):
                    sp.dma_start(e_attn[:, c, :], attn_scr[bass.ds(b, 1), c * P:(c + 1) * P, bass.ds(tc * CH, CH)].rearrange("o p t -> p (o t)")).then_inc(e_loaded, DMA)
                sp.dma_start(e_x[:, :, :], x[bass.ds(b, 1), bass.ds(tc * CH, CH), :].rearrange("o (n p) e -> p (o n) e", p=P)).then_inc(e_loaded, DMA)

            def e_modulation(b):
                for c in range(EC):
                    sp.dma_start(e_cols[:, :, c], mod_scr[bass.ds(b, 1), 3:5, c * P:(c + 1) * P].rearrange("o k p -> p (o k)"), allow_slow_non_contiguous=True).then_inc(e_mod_loaded, DMA)
                for i, kind in enumerate((2, 5)):
                    sp.dma_start(e_gate[:, i, :], mod_scr[bass.ds(b, 1), kind, :].broadcast_to([P, E])).then_inc(e_mod_loaded, DMA)

            def e_store(b, tc, evacuated):
                sp.wait_ge(e_evacuated, evacuated)
                sp.dma_start(out[bass.ds(b, 1), bass.ds(tc * CH, CH), :].rearrange("o (n p) e -> p (o n) e", p=P), e_y[:, :, :]).then_inc(e_stored, DMA)

            def rows_of(b, g, buf, loaded):
                for half in range(2):
                    for r, (qp, kp) in enumerate(QK_ROWS):
                        at = 64 * half + HD * r
                        for tile, scr, part in ((queries[buf], q_scr, qp), (keys[buf], k_scr, kp)):
                            src = scr[bass.ds(b, 1), part, bass.ds(g * 4 * HD + half * 2 * HD, 2 * HD), :]
                            sp.dma_start(tile[at:at + HD, :, :], src.rearrange("o (s d) t -> d (o s) t", d=HD)).then_inc(loaded, DMA)

            def group_rows(b, g, buf):
                rows_of(b, g, buf, group_loaded[buf])
                src = v_scr[bass.ds(b, 1), bass.ds(g, 1), :, :, :]
                sp.dma_start(values[buf][:, :, :, :].rearrange("p n h w -> p n (h w)"),
                             src.rearrange("o u p n w -> p (o u n) w")).then_inc(group_loaded[buf], DMA)

            def maxima_rows(b, g, buf, loaded):
                for half in range(2):
                    at = 64 * half + KQ
                    src = m_scr[bass.ds(b, 1), :, bass.ds(g * 4 + half * 2, 2), :]
                    sp.dma_start(queries[buf][at:at + PARTS, :, :], src.rearrange("o i s t -> (o i) s t")).then_inc(loaded, DMA)

            def group_maxima(b, g, buf):
                maxima_rows(b, g, buf, group_loaded[buf])

            def m_store(b, done, value, stored):
                wait_alone(sp, done, value, sp_passed)
                sp.dma_start(m_scr[bass.ds(b, 1), :, :, :].rearrange("o i s t -> s (o i) t"), m_parts[:, :, :]).then_inc(stored, DMA)

            sp.dma_start(c_sb[:, :, :], cT.rearrange("(c p) b -> p c b", p=P)).then_inc(small_loaded, DMA)
            for i, v in enumerate((lq1, lk1, lq2, lk2)):
                sp.dma_start(lam_in[:, i, :], v.rearrange("(o d) -> o d", o=1).broadcast_to([P, HD])).then_inc(small_loaded, DMA)
            sp.dma_start(subln_sb[:, :], subln.rearrange("(o d) -> o d", o=1).broadcast_to([64, VD])).then_inc(small_loaded, DMA)
            sp.dma_start(wmod_sb[:, :, :], wmod.rearrange("(c p) f -> p c f", p=P)).then_inc(wmod_loaded, DMA)
            a_load(0, 0)
            for w, src in ((wf, wfT), (wq, wqT), (wk, wkT), (wv, wvT), (wo, woT)):
                sp.dma_start(w[:, :, :], src.rearrange("(c p) f -> p c f", p=P)).then_inc(weights_loaded, DMA)
            sp.wait_ge(mod_done, 1)
            sp.dma_start(mod_scr, mod_sb[:, :, :]).then_inc(mod_stored, DMA)
            sp.wait_ge(mod_stored, DMA)
            a_columns(0)
            sp.wait_ge(a_normed, 1)
            a_load(0, 1)
            with sp.Fori(0, NC) as tc:
                a_wait(tc)
                a_store_qk(tc, 0, tc, 0)
                with sp.If(tc < NC - 2):
                    sp.wait_ge(a_normed, tc + 2)
                    a_load(0, inside(tc + 2, NC - 1, "inside If(tc < NC - 2)"))
                for i in range(1, 4):
                    a_store_qk(tc, 0, tc, i)
                a_store_v(tc, 0, tc)
            a_columns(1)
            a_load(1, 0)
            a_wait(NC)
            group_rows(0, 0, 0)
            m_store(0, m_done, 1, m_stored)
            sp.wait_ge(m_stored, DMA)
            group_maxima(0, 0, 0)
            exact_runs = sp.alloc_register("sp_exact_runs")
            sp.reg_mov(exact_runs, 0)

            with sp.Fori(0, B) as b:
                wait_alone(sp, m_flag_set, b + 1, sp_passed)
                exact = sp.value_load(m_flag[0:1, 0:1], min_val=0, max_val=1)
                with sp.If(exact > 0):
                    runs = sp.snap(exact_runs, min_val=0, max_val=B - 1)
                    wait_alone(sp, group_loaded[0], (b * GP + 1) * (GROUP_LOADS * DMA), sp_passed)
                    with sp.Fori(0, NG) as g:
                        rows_of(b, g, 0, m_rows_loaded)
                        wait_alone(sp, m_scores, (runs * NG + g + 1) * (4 * NB), sp_passed)
                    rows_of(b, 0, 0, m_rows_loaded)
                    m_store(b, exact_done, runs + 1, m_rows_loaded)
                    wait_alone(sp, m_rows_loaded, (runs + 1) * (EXACT_LOADS * DMA) - 2 * DMA, sp_passed)
                    maxima_rows(b, 0, 0, m_rows_loaded)
                    wait_alone(sp, m_rows_loaded, (runs + 1) * (EXACT_LOADS * DMA), sp_passed)
                    sp.reg_add(exact_runs, exact_runs, 1)
                with sp.Fori(0, GP) as gp:
                    body = b * GP + gp
                    ejob = (body + (B - 1) * GP) % (B * GP)
                    after, before = (b + 1) % B, (b + B - 1) % B
                    group_rows(b, gp * 2 + 1, 1)
                    group_maxima(b, gp * 2 + 1, 1)
                    with sp.If(b > 0):
                        with sp.If(gp == 0):
                            e_modulation(before)
                        e_loads(before, gp)
                    for s in range(SEGS):
                        if s in (1, 2):
                            with sp.If(b < B - 1):
                                a_store_qk(body + NC, after, gp, 2 * (s - 1))
                                a_store_qk(body + NC, after, gp, 2 * (s - 1) + 1)
                        if s == 3:
                            with sp.If(b < B - 1):
                                a_store_v(body + NC, after, gp)
                        if s == 7:
                            with sp.If(b < B - 1):
                                with sp.If(gp == GP - 1):
                                    m_store(after, m_done, b + 2, m_stored)
                                    sp.wait_ge(m_stored, (b + 2) * DMA)
                                    group_maxima(after, 0, 0)
                        if s == 6:
                            with sp.If(body == B * GP - 1):
                                wait_alone(sp, e_evacuated, ejob * E_STEPS + 2, sp_passed)
                                wait_alone(sp, seg_stored, (body * SEGS + s) * DMA, sp_passed)
                                e_loads(B - 1, 0)
                        if s == 7:
                            with sp.If(b > 0):
                                e_store(before, gp, (ejob + 1) * E_STEPS)
                            with sp.If(body == B * GP - 1):
                                e_modulation(B - 1)
                            with sp.If(b < B - 1):
                                with sp.If(gp < GP - 1):
                                    a_load(after, inside(gp + 1, NC - 1, "inside If(gp < GP - 1)"))
                            with sp.If(b < B - 2):
                                with sp.If(gp == GP - 1):
                                    a_columns((b + 2) % B)
                                    a_load((b + 2) % B, 0)
                        sp.wait_ge(seg_done, body * SEGS + s + 1)
                        sp.dma_start(attn_scr[bass.ds(b, 1), bass.ds((gp * 2 + s // NC) * 32, 32), (s % NC) * CH:(s % NC + 1) * CH].rearrange("o p t -> p (o t)"),
                                     seg_o[:, :]).then_inc(seg_stored, DMA)
                        if s == NC:
                            with sp.If(gp < GP - 1):
                                sp.wait_ge(pv_done, PRING + body * BODY + UNITS)
                                g = inside(gp * 2 + 2, NG - 1, "inside If(gp < GP - 1)")
                                group_rows(b, g, 0)
                                group_maxima(b, g, 0)
                            with sp.If(b < B - 1):
                                a_wait(body + NC + 1)
                                with sp.If(gp == GP - 1):
                                    sp.wait_ge(pv_done, PRING + body * BODY + UNITS)
                                    group_rows(after, 0, 0)
                wait_alone(sp, seg_stored, (b + 1) * (GP * SEGS * DMA), sp_passed)

            for k, (tc, i) in enumerate(LAST_E):
                if i == 1 and tc < NC - 1:
                    sp.wait_ge(e_evacuated, LAST_JOB * E_STEPS + k + 1)
                    e_loads(B - 1, tc + 1)
                if i == 5:
                    e_store(B - 1, tc, LAST_JOB * E_STEPS + k + 1)
            sp.wait_ge(e_stored, (B * NC + 1) * DMA)

        @block.gpsimd
        def _(pool):
            nc.gpsimd.memset(ones[:, :], 1.0).then_inc(consts_set, 1)
            nc.gpsimd.memset(neg_half[:, :], -0.5).then_inc(consts_set, 1)
            nc.gpsimd.memset(ident[:, :], 0.0).then_inc(ident_set, 1)
            pool.wait_ge(ident_set, 1)
            nc.gpsimd.affine_select(out=ident[:, :], in_=ident[:, :], compare_op=ALU.not_equal, fill=1.0, base=0,
                                    pattern=[[-1, P]], channel_multiplier=1).then_inc(ident_set, 1)
            for buf in range(2):
                nc.gpsimd.memset(keys[buf][:, :, :], 1.0).then_inc(consts_set, 1)
                nc.gpsimd.memset(queries[buf][:, :, :], 0.0).then_inc(consts_set, 1)
            nc.gpsimd.memset(head_mask[:, :], 1.0).then_inc(ident_set, 1)
            pool.wait_ge(ident_set, 3)
            nc.gpsimd.affine_select(out=head_mask[:, :], in_=head_mask[:, :], compare_op=ALU.is_ge, fill=0.0, base=0,
                                    pattern=[[-HD, NS // EC]], channel_multiplier=1).then_inc(ident_set, 1)
            pool.wait_ge(ident_set, 4)
            nc.gpsimd.affine_select(out=head_mask[:, :], in_=head_mask[:, :], compare_op=ALU.is_ge, fill=0.0, base=HD - 1,
                                    pattern=[[HD, NS // EC]], channel_multiplier=-1).then_inc(ident_set, 1)
            nc.gpsimd.memset(a_v[:, :, :, :, :], 0.0).then_inc(consts_set, 1)
            pool.wait_ge(consts_set, 7)
            nc.gpsimd.memset(a_v[:, :, :, :, VD:VD + 1], 1.0).then_inc(consts_set, 1)

            def a_power(job):
                pool.wait_ge(a_var, job + 1)
                nc.gpsimd.tensor_tensor(a_rstd[:, :], a_ve[:, :], neg_half[:, 0:BPC], ALU.pow).then_inc(a_rstd_done, 1)

            def a_split_parts(job, i):
                src = a_qk[:, i, :]
                link = Chain(pool, a_pool_chain, (job - NC) * 12 + i * 3, pool_passed)
                wait_alone(pool, a_evacuated, job * A_STEPS + 3 + i, pool_passed)
                if i == 0:
                    wait_alone(pool, a_stored, (job + 1) * A_STORES * DMA, pool_passed)
                link.then(nc.gpsimd.tensor_copy(a_parts[:, i, 0, :], src))
                link.then(nc.gpsimd.tensor_tensor(a_rest[:, :], src, a_parts[:, i, 0, :], ALU.subtract))
                link.then(nc.gpsimd.tensor_copy(a_parts[:, i, 1, :], a_rest[:, :]))
                nc.gpsimd.tensor_tensor(a_parts[:, i, 2, :], a_rest[:, :], a_parts[:, i, 1, :], ALU.subtract).then_inc(a_split, 1)
                wait_alone(pool, a_split, (job + 1) * 4 + i + 1, pool_passed)

            def a_split_with_scalar(job, i):
                src = a_qk[:, i, :]
                wait_alone(pool, a_head, job * 4 + i + 1, pool_passed)
                nc.gpsimd.tensor_tensor(a_rest[:, :], src, a_parts[:, i, 0, :], ALU.subtract).then_inc(a_rest_done, 1)
                wait_alone(pool, a_middle, job * 4 + i + 1, pool_passed)
                nc.gpsimd.tensor_tensor(a_parts[:, i, 2, :], a_rest[:, :], a_parts[:, i, 1, :], ALU.subtract).then_inc(a_split, 1)
                wait_alone(pool, a_split, (job + 1) * 4 + i + 1, pool_passed)

            def e_power(job):
                pool.wait_ge(e_var, job + 1)
                nc.gpsimd.tensor_tensor(e_rstd[:, :], e_ve[:, :], neg_half[:, 0:BPC], ALU.pow).then_inc(e_rstd_done, 1)

            a_power(0)
            with pool.Fori(0, NC) as tc:
                with pool.If(tc < NC - 1):
                    a_power(tc + 1)
                for i in range(4):
                    a_split_with_scalar(tc, i)
            with pool.Fori(0, B) as b:
                with pool.Fori(0, GP) as gp:
                    body = b * GP + gp
                    ejob = (body + (B - 1) * GP) % (B * GP)
                    with pool.If(b < B - 1):
                        a_power(body + NC)
                    for s in range(SEGS):
                        if s in (1, 2):
                            with pool.If(b < B - 1):
                                a_split_parts(body + NC, 2 * (s - 1))
                                a_split_parts(body + NC, 2 * (s - 1) + 1)
                        if s == A_STEPS // 2:
                            with pool.If(b > 0):
                                e_power(ejob)
                        pool.wait_ge(seg_ms_done, body * SEGS + s + 1)
                        nc.gpsimd.tensor_tensor(seg_rs[:, :], seg_ms[:, :], neg_half[0:64, :], ALU.pow).then_inc(seg_rs_done, 1)
            with pool.Fori(0, NC) as tc:
                e_power((B - 1) * NC + tc)

        @block.scalar
        def _(act):
            act.wait_ge(small_loaded, 6 * DMA)
            nc.scalar.activation(c_exp[:, :, :], c_sb[:, :, :], ACT.Exp, scale=-1.0).then_inc(c_exp_done, 1)
            act.wait_ge(lam_sum_done, 1)
            nc.scalar.activation(lam_exp[:, :], lam_sum[:, :], ACT.Exp).then_inc(lam_exp_done, 1)
            nc.scalar.activation(act_open[:, :], lam_sum[:, :], ACT.Exp).then_inc(exp_done, SLOTS)
            with act.Fori(0, NC) as tc:
                for i in range(4):
                    act.wait_ge(a_evacuated, tc * A_STEPS + 3 + i)
                    if i == 0:
                        act.wait_ge(a_stored, (tc + 1) * A_STORES * DMA)
                    nc.scalar.activation(a_parts[:, i, 0, :], a_qk[:, i, :], ACT.Copy).then_inc(a_head, 1)
                    act.wait_ge(a_rest_done, tc * 4 + i + 1)
                    nc.scalar.activation(a_parts[:, i, 1, :], a_rest[:, :], ACT.Copy).then_inc(a_middle, 1)
            with act.Fori(0, B * GP) as body:
                for n in range(2 * BODY):
                    u = n // PAIRS
                    act.wait_ge(scores_ready, body * (2 * BODY) + n + 1)
                    if n % PAIRS == 0:
                        act.wait_ge(pv_done, body * BODY + u + 1)
                    nc.scalar.activation(probs[:, u % PRING, n % PAIRS, :, :], slots[slot_of(n)], ACT.Exp).then_inc(exp_done, 1)

        @block.tensor
        def _(pe):
            pe.wait_ge(wmod_loaded, DMA)
            pe.wait_ge(silu_done, 1)
            for k in range(3):
                for c in range(EC):
                    last = nc.tensor.matmul(ps[0:B, k, :], silu[:, c, :], wmod_sb[:, c, k * 512:(k + 1) * 512], start=(c == 0), stop=(c == EC - 1))
            last.then_inc(mod_product, 1)
            pe.wait_ge(weights_loaded, 5 * DMA)
            pe.wait_ge(w_sum_done, 1)
            pe.wait_ge(consts_set, 8)
            nc.tensor.matmul(ps[:, 3, 0:1], ones[:, :], w_sum[:, :], start=True, stop=True).then_inc(w_total, 1)
            pe.wait_ge(ident_set, 2)
            pe.wait_ge(setup_done, 1)

            def transposes(src, c, bank):
                for n in range(BPC):
                    last = nc.tensor.transpose(bank[:, n * P:(n + 1) * P], src[:, n, c * P:(c + 1) * P], ident[:, :])
                return last

            def token_products(hT, w, n0, bank):
                for n in range(n0, n0 + 2):
                    for c in range(EC):
                        last = nc.tensor.matmul(bank[:, (n - n0) * E:(n - n0 + 1) * E], hT[:, c, n * P:(n + 1) * P], w[:, c, :],
                                                start=(c == 0), stop=(c == EC - 1))
                return last

            def a_step(job, i, ahead=False):
                bank = ps[:, i, :] if ahead else aux
                if i == 0:
                    pe.wait_ge(a_normed, job + 1)
                elif i == 2 or not ahead:
                    pe.wait_ge(a_evacuated, job * A_STEPS + i)
                if i < 2:
                    last = transposes(normed, i, bank)
                elif i < 6:
                    w = (wq, wk)[(i - 2) // 2]
                    f = (i - 2) % 2
                    for c in range(EC):
                        last = nc.tensor.matmul(bank, w[:, c, f * P:(f + 1) * P], a_hT[:, c, :], start=(c == 0), stop=(c == EC - 1))
                else:
                    last = token_products(a_hT, wv, (i - 6) * 2, bank)
                last.then_inc(a_product, 1)

            def e_step(job, i, bank=aux, place=None):
                if i == 0:
                    pe.wait_ge(e_loaded, (job + 1) * 3 * DMA)
                if place is None:
                    if i == 0:
                        pe.wait_ge(e_open, job + 1)
                    else:
                        pe.wait_ge(e_evacuated, job * E_STEPS + i)
                elif place == 0:
                    pe.wait_ge(e_evacuated, LAST_JOB * E_STEPS)
                elif place == 1:
                    pe.wait_ge(pv_read, B * GP * SEGS + 1)
                else:
                    hT = LAST_E.index((job - LAST_JOB, 3)) + 1 if i == 4 else 0
                    pe.wait_ge(e_evacuated, LAST_JOB * E_STEPS + max(place - 1, hT))
                if i < 2:
                    last = token_products(e_attn, wo, i * 2, bank)
                elif i < 4:
                    pe.wait_ge(e_normed, job + 1)
                    last = transposes(normed, i - 2, bank)
                else:
                    last = token_products(e_hT, wf, (i - 4) * 2, bank)
                last.then_inc(e_product, 1)

            def m_transposes(k):
                for n in range(BPC):
                    last = nc.tensor.transpose(aux[0:NS, n * P:(n + 1) * P], m_cols[:, k * BPC + n, :], ident[:, :])
                return last

            def m_step(m, i, bank=aux):
                if i == 0:
                    pe.wait_ge(m_open, m + 1)
                if i < 8:
                    for blk in (2 * i, 2 * i + 1):
                        for c in range(EC):
                            at = (blk % 2) * (NS * BOX) + c * (NS // EC) * BOX
                            for sign in range(2):
                                last = nc.tensor.matmul(bank[:, at:at + (NS // EC) * BOX], q_sign[:, c, sign, blk * P:(blk + 1) * P],
                                                        box_w[:, c, sign, :, :].rearrange("p h k -> p (h k)"), start=(sign == 0), stop=(sign == 1))
                elif i == 8:
                    pe.wait_ge(m_crit_done, m + 1)
                    last = nc.tensor.transpose(aux[0:1, 0:P], m_crit[:, 0:1], ident[:, :])
                else:
                    last = m_transposes(i - 9)
                last.then_inc(m_product, 1)

            def scores(body, u, n):
                buf, tc, blk = u // UNITS, u // NB % NC, u % NB
                pe.wait_ge(exp_done, body * (2 * BODY) + n + 1 + (n in (1, 2 * BODY - 1)))
                for half in range(2):
                    at = 64 * half
                    last = nc.tensor.matmul(slots[slot_of(n)][:, half, :], keys[buf][at:at + KS_ROWS, n % PAIRS, blk * P:(blk + 1) * P],
                                            queries[buf][at:at + KS_ROWS, n % PAIRS, tc * CH:(tc + 1) * CH], start=True, stop=True)
                last.then_inc(scores_ready, 1)

            def weighted(body, u):
                buf, blk, seg = u // UNITS, u % NB, u // NB
                if blk == 0:
                    pe.wait_ge(pv_read, body * SEGS + seg + 1)
                pe.wait_ge(exp_done, SLOTS + body * (2 * BODY) + PAIRS * (u + 1))
                for pair in range(PAIRS):
                    for half in range(2):
                        j = 32 * (2 * pair + half)
                        last = nc.tensor.matmul(pv[j:j + VW, :], values[buf][:, blk, half, :], probs[:, u % PRING, pair, half, :],
                                                start=(blk == 0), stop=(blk == NB - 1))
                last.then_inc(pv_done, 1)

            with pe.Fori(0, NC) as tc:
                for i in range(A_STEPS):
                    a_step(tc, i, ahead=True)
            pe.wait_ge(a_evacuated, NC * A_STEPS)
            for i in range(M_STEPS):
                if i >= 8:
                    pe.wait_ge(m_evacuated, i)
                m_step(0, i, ps[:, i % 8, :])

            exact_runs = pe.alloc_register("pe_exact_runs")
            pe.reg_mov(exact_runs, 0)
            behind = pe.alloc_register("pe_behind")
            pe.reg_mov(behind, 0)
            with pe.Fori(0, B) as b:
                wait_alone(pe, m_flag_set, b + 1, pe_passed)
                exact = pe.value_load(m_flag[0:1, 0:1], min_val=0, max_val=1)
                with pe.If(exact > 0):
                    with pe.If(b > 0):
                        for u in range(BODY - LAG, BODY):
                            weighted(b * GP - 1, u)
                        pe.reg_mov(behind, 0)
                    runs = pe.snap(exact_runs, min_val=0, max_val=B - 1)
                    wait_alone(pe, m_evacuated, (b + 1) * M_STEPS, pe_passed)
                    wait_alone(pe, pv_read, b * (GP * SEGS) + 1, pe_passed)
                    with pe.Fori(0, NG) as g:
                        pe.wait_ge(m_rows_loaded, (runs * EXACT_LOADS + (g + 1) * ROW_LOADS) * DMA)
                        for n in range(4 * NB):
                            head, blk = n // NB, n % NB
                            pair, at = head // 2, 64 * (head % 2)
                            pe.wait_ge(m_reduced, (runs * NG + g) * (4 * NB) + n + 1)
                            for k in range(NC):
                                last = nc.tensor.matmul(ps[:, 4 * (n % 2) + k, :], queries[0][at:at + KQ, pair, blk * P:(blk + 1) * P],
                                                        keys[0][at:at + KQ, pair, k * CH:(k + 1) * CH], start=True, stop=True)
                            last.then_inc(m_scores, 1)
                    wait_alone(pe, m_reduced, (runs + 1) * NG * (4 * NB) + 2, pe_passed)
                    for k in range(NC):
                        if k > 0:
                            pe.wait_ge(exact_evacuated, runs * NC + k)
                        m_transposes(k).then_inc(exact_product, 1)
                    wait_alone(pe, exact_evacuated, (runs + 1) * NC, pe_passed)
                    wait_alone(pe, m_rows_loaded, (runs + 1) * (EXACT_LOADS * DMA), pe_passed)
                    pe.reg_add(exact_runs, exact_runs, 1)

                with pe.Fori(0, GP) as gp:
                    body = b * GP + gp
                    ejob = (body + (B - 1) * GP) % (B * GP)
                    for u in range(BODY):
                        if u % UNITS == 0:
                            buf = u // UNITS
                            pe.wait_ge(group_loaded[buf], (body + 1) * (GROUP_LOADS * DMA))
                        for n in (PAIRS * u, PAIRS * u + 1):
                            scores(body, u, n)
                        if u >= LAG:
                            weighted(body, u - LAG)
                        else:
                            with pe.If(pe.snap(behind, min_val=0, max_val=1) > 0):
                                weighted(body - 1, BODY - LAG + u)
                        if u in M_UNITS:
                            i = M_UNITS[u]
                            with pe.If(b < B - 1):
                                with pe.If(gp == GP - 1):
                                    if i > 0:
                                        pe.wait_ge(m_evacuated, (b + 1) * M_STEPS + i)
                                    if i in (0, 3):
                                        pe.wait_ge(a_evacuated, (body + NC) * A_STEPS + (7 if i == 0 else 8))
                                    if i in (3, 6, 9, 11):
                                        with pe.If(b > 0):
                                            pe.wait_ge(e_evacuated, ejob * E_STEPS + {3: 1, 6: 3, 9: 5, 11: 6}[i])
                                    m_step(b + 1, i)
                        if u in STEP_UNITS:
                            i = STEP_UNITS.index(u)
                            if i % 2 == 1 and i // 2 in M_GROUPS:
                                with pe.If(b < B - 1):
                                    with pe.If(gp == GP - 1):
                                        pe.wait_ge(m_evacuated, (b + 1) * M_STEPS + M_GROUPS[i // 2][-1] + 1)
                            if i < A_STEPS:
                                with pe.If(b < B - 1):
                                    a_step(body + NC, i)
                            elif i < A_STEPS + E_STEPS:
                                with pe.If(b > 0):
                                    e_step(ejob, i - A_STEPS)
                    pe.reg_mov(behind, 1)
            for u in range(BODY - LAG, BODY):
                weighted(B * GP - 1, u)

            for k, (tc, i) in enumerate(LAST_E):
                e_step(LAST_JOB + tc, i, (aux, pv)[k % 2], k)

        @block.vector
        def _(dve):
            V = nc.vector

            def norm_stats(link, src, ve, var_sem):
                for n in range(BPC):
                    last = V.bn_stats(stats[:, n, :], src[:, n, :])
                link.then(last)
                dve.sem_inc(dve_passed, 1)
                for n in range(BPC):
                    last = V.bn_aggr(moments[:, n, :], stats[:, n, :])
                link.then(last)
                V.tensor_scalar(ve[:, :], moments[:, :, 1], EPS, None, ALU.add).then_inc(var_sem, 1)

            def norm_apply(src, rstd, rstd_sem, job, done):
                dve.wait_ge(rstd_sem, job + 1)
                for n in range(BPC):
                    last = V.tensor_scalar(normed[:, n, :], src[:, n, :], moments[:, n, 0:1], rstd[:, n:n + 1], ALU.subtract, ALU.mult)
                last.then_inc(done, 1)

            def a_stats(job):
                dve.wait_ge(a_loaded, (job + 1) * DMA)
                norm_stats(Chain(dve, a_chain, job * 2), a_x, a_ve, a_var)

            def a_apply(job):
                norm_apply(a_x, a_rstd, a_rstd_done, job, a_normed)

            link = Chain(dve, start_chain, 0)
            dve.wait_ge(c_exp_done, 1)
            link.then(V.tensor_scalar(c_exp[:, :, :], c_exp[:, :, :], 1.0, None, ALU.add))
            link.then(V.reciprocal(c_exp[:, :, :], c_exp[:, :, :]))
            V.tensor_tensor(silu[:, :, :], c_sb[:, :, :], c_exp[:, :, :], ALU.mult).then_inc(silu_done, 1)
            lam4 = lam_in[:, :, :].rearrange("p (i j) d -> p i j d", j=2)
            link.then(V.tensor_tensor(lam_prod[:, :, :], lam4[:, :, 0, :], lam4[:, :, 1, :], ALU.mult))
            V.tensor_reduce(lam_sum[:, :], lam_prod[:, :, :], axis=AX.X, op=ALU.add).then_inc(lam_sum_done, 1)
            dve.wait_ge(weights_loaded, 5 * DMA)
            V.tensor_reduce(w_sum[:, :], wf[:, :, :], axis=AX.XY, op=ALU.add, apply_absolute_value=True).then_inc(w_sum_done, 1)
            dve.wait_ge(lam_exp_done, 1)
            link.then(V.tensor_scalar(coef[:, :], lam_exp[:, 1:2], lam_exp[:, 0:1], -LAMBDA_INIT, ALU.subtract, ALU.add))
            link.then(V.memset(coef[0:64, :], 1.0))
            a_stats(0)
            a_apply(0)
            dve.wait_ge(mod_product, 1)
            link.then(V.tensor_copy(mod_sb[:, :, :].rearrange("b k e -> b (k e)"), ps[0:B, 0:3, :].rearrange("b k e -> b (k e)")))
            for kind in (1, 4):
                V.tensor_scalar(mod_sb[:, kind, :], mod_sb[:, kind, :], 1.0, None, ALU.add)
            for kind in (2, 5):
                link.then(V.scalar_tensor_tensor(gate_abs[:, :], mod_sb[:, kind, :], -1.0, mod_sb[:, kind, :], ALU.mult, ALU.max))
                V.tensor_scalar(gate_abs[:, :], gate_abs[:, :], 0.25, None, ALU.max)
                link.then(V.tensor_scalar(gate_sign[:, :], mod_sb[:, kind, :], 0.0, 2.0, ALU.is_ge, ALU.mult))
                link.then(V.scalar_tensor_tensor(mod_sb[:, kind, :], gate_sign[:, :], -1.0, gate_abs[:, :], ALU.add, ALU.mult))
            V.tensor_copy(e_open_t[0:B, :], mod_sb[:, 0, 0:1]).then_inc(mod_done, 1)
            dve.wait_ge(w_total, 1)
            link.then(V.tensor_scalar(w_scale[:, :], ps[:, 3, 0:1], 1.0 / (E * E), 1e-5, ALU.mult, ALU.max))
            V.tensor_scalar(w_half[:, 0:1], w_scale[:, :], 0.5, None, ALU.mult)
            link.then(V.tensor_scalar(w_half[:, 1:2], w_scale[:, :], -0.5, None, ALU.mult))
            V.tensor_scalar(w_low[:, :, :], wf[:, :, :], w_half[:, 1:2], w_scale[:, :], ALU.is_lt, ALU.mult)
            link.then(V.tensor_scalar(wf[:, :, :], wf[:, :, :], w_half[:, 0:1], w_scale[:, :], ALU.is_gt, ALU.mult))
            link.then(V.tensor_tensor(wf[:, :, :], wf[:, :, :], w_low[:, :, :], ALU.subtract))
            V.memset(e_open_t[:, :], 0.0).then_inc(pv_read, 1)
            link.then(V.memset(seg_r[:, :], 0.0))
            V.memset(seg_rc[:, :], 0.0).then_inc(m_reduced, 2)
            V.memset(m_worst[:, :], 0.0).then_inc(a_split, 4)
            V.memset(seg_t[:, :, :], 0.0).then_inc(pv_done, PRING)
            V.memset(seg_ss[:, :], 0.0).then_inc(a_stored, A_STORES * DMA)
            V.memset(m_size[:, 0, :], 0.0).then_inc(e_stored, DMA)
            V.memset(stats[:, 0, :], 0.0).then_inc(setup_done, 1)
            dve.wait_ge(setup_done, 1)

            def a_bounds(job, i, tc):
                c = i % 2
                wait_alone(dve, a_evacuated, job * A_STEPS + 3 + i, dve_passed)
                src, at = a_qk[:, i, :], bass.ds(tc, 1)
                if i < 2:
                    for sign, op in enumerate((ALU.max, ALU.min)):
                        V.tensor_scalar(q_sign[:, c, sign, bass.ds(tc * CH, CH)], src, 0.0, None, op)
                    last = V.tensor_reduce(a_qabs[:, c, at], src, axis=AX.X, op=ALU.max, apply_absolute_value=True)
                else:
                    V.tensor_reduce(box[:, c, 0, at], src, axis=AX.X, op=ALU.max)
                    V.tensor_reduce(box[:, c, 1, at], src, axis=AX.X, op=ALU.min)
                    last = V.tensor_reduce(a_sum[:, c, at], src, axis=AX.X, op=ALU.add)
                last.then_inc(a_bounded, 1)
                wait_alone(dve, a_bounded, job * 4 + i + 1, dve_passed)

            def a_evacuate(job, i, m, tc, bank=aux):
                if i == 0:
                    wait_alone(dve, a_cols_loaded, (m + 1) * EC * DMA, dve_passed)
                if 2 <= i < 6:
                    wait_alone(dve, a_split, job * 4 + i - 1, dve_passed)
                if i == 6:
                    wait_alone(dve, a_stored, (job + 1) * A_STORES * DMA, dve_passed)
                dve.wait_ge(a_product, job * A_STEPS + i + 1)
                if i < 2:
                    last = V.tensor_scalar(a_hT[:, i, :], bank, a_cols[:, 1, i:i + 1], a_cols[:, 0, i:i + 1], ALU.mult, ALU.add)
                elif i < 6:
                    last = V.tensor_scalar(a_qk[:, i - 2, :], bank, SCALING if i < 4 else 1.0, None, ALU.mult)
                else:
                    for n in range(2):
                        last = V.tensor_copy(a_v[:, :, (i - 6) * 2 + n, :, 0:VD], bank[:, n * E:(n + 1) * E].rearrange("p (g h d) -> p g h d", g=NG, h=2))
                last.then_inc(a_evacuated, 1)
                if 2 <= i < 6:
                    a_bounds(job, i - 2, tc)

            def e_evacuate(job, i, m, bank=aux, place=None, link=None, x2=e_x2):
                count = job * E_STEPS + i if place is None else LAST_JOB * E_STEPS + place
                if i == 0:
                    wait_alone(dve, e_loaded, (job + 1) * 3 * DMA, dve_passed)
                    wait_alone(dve, e_mod_loaded, (m + 1) * 4 * DMA, dve_passed)
                    if place is None:
                        V.tensor_copy(e_open_t[:, :], e_cols[:, 0, 0:1]).then_inc(e_open, 1)
                if i == 4:
                    wait_alone(dve, e_stored, (job + 1) * DMA, dve_passed)
                link = link or Chain(dve, e_chain, job * E_LINKS + (0, 1, 4, 4, 4, 5)[i])
                dve.wait_ge(e_product, count + 1)
                two = bank.rearrange("p (n e) -> p n e", n=2)
                n0 = (i % 2) * 2
                if i in (2, 3):
                    V.tensor_scalar(e_hT[:, i - 2, :], bank, e_cols[:, 1, i - 2:i - 1], e_cols[:, 0, i - 2:i - 1], ALU.mult, ALU.add).then_inc(e_evacuated, 1)
                    return
                gate, base, dst = (0, e_x, x2) if i < 2 else (1, x2, e_y)
                link.then(V.tensor_tensor(e_tmp[:, :, :], two, e_gate[:, gate:gate + 1, :].broadcast_to([P, 2, E]), ALU.mult))
                V.tensor_tensor(dst[:, n0:n0 + 2, :], e_tmp[:, :, :], base[:, n0:n0 + 2, :], ALU.add).then_inc(e_evacuated, 1)
                wait_alone(dve, e_evacuated, count + 1, dve_passed)
                if i == 1:
                    norm_stats(link, x2, e_ve, e_var)
                    norm_apply(x2, e_rstd, e_rstd_done, job, e_normed)

            def segment(body, s):
                NQ = CH // 32
                link = Chain(dve, s_chain, (body * SEGS + s) * S_LINKS)
                if s:
                    wait_alone(dve, seg_stored, (body * SEGS + s) * DMA, dve_passed)
                else:
                    with dve.If(body > 0):
                        wait_alone(dve, seg_stored, body * (SEGS * DMA), dve_passed)
                dve.wait_ge(pv_done, PRING + body * BODY + (s + 1) * NB)
                V.transpose(seg_t[:, :, :].rearrange("p c d -> p (c d)"), pv).then_inc(pv_read, 1)
                dve.wait_ge(pv_read, body * SEGS + s + 2)
                link.then(V.reciprocal(seg_r[:, :], seg_t[:, :, VD]))
                link.then(V.tensor_scalar(seg_rc[:, :], seg_r[:, :], coef[:, 0:1], None, ALU.mult))
                link.then(V.tensor_tensor(seg_w[:, :, :], seg_t[:, :, 0:VD], seg_rc[:, :].rearrange("p (c o) -> p c o", o=1).broadcast_to([P, NQ, VD]), ALU.mult))
                link.then(V.tensor_copy(seg_w2[:, :, :], seg_w[64:128, :, :]))
                link.then(V.tensor_tensor(seg_d[:, :, :], seg_w[0:64, :, :], seg_w2[:, :, :], ALU.add))
                link.then(V.tensor_tensor(seg_sq[:, :, :], seg_d[:, :, :], seg_d[:, :, :], ALU.mult))
                link.then(V.tensor_reduce(seg_ss[0:64, :], seg_sq[:, :, :], axis=AX.X, op=ALU.add))
                V.tensor_scalar(seg_ms[:, :], seg_ss[0:64, :], 1.0 / VD, EPS, ALU.mult, ALU.add).then_inc(seg_ms_done, 1)
                dve.wait_ge(seg_rs_done, body * SEGS + s + 1)
                V.tensor_tensor(seg_n[:, :, :], seg_d[:, :, :], seg_rs[:, :].rearrange("p (c o) -> p c o", o=1).broadcast_to([64, NQ, VD]), ALU.mult).then_inc(s_chain_n, 1)
                dve.wait_ge(s_chain_n, (body * SEGS + s) * 2 + 1)
                for h in range(2):
                    q = slice(32 * h, 32 * h + 32)
                    last = V.scalar_tensor_tensor(seg_a[:, :, h * VD:(h + 1) * VD], seg_n[q, :, :], 1.0 - LAMBDA_INIT,
                                                  subln_sb[q, :].rearrange("p (o d) -> p o d", o=1).broadcast_to([32, NQ, VD]), ALU.mult, ALU.mult)
                last.then_inc(s_chain_n, 1)
                dve.wait_ge(s_chain_n, (body * SEGS + s) * 2 + 2)
                V.transpose(seg_o[:, :], seg_a[:, :, :].rearrange("p c d -> p (c d)")).then_inc(seg_done, 1)

            HH = NS // EC

            def m_prepare(m):
                link = Chain(dve, m_chain, m * M_LINKS, dve_passed)
                link.then(V.tensor_reduce(m_mean[:, :], a_sum[:, :, :], axis=AX.X, op=ALU.add))
                for sign in range(2):
                    last = V.tensor_scalar(box[:, :, sign, NC], m_mean[:, :], 1.0 / T, None, ALU.mult)
                link.then(last)
                for c in range(EC):
                    for sign in range(2):
                        last = V.tensor_tensor(box_w[:, c, sign, :, :], head_mask[:, :].rearrange("p (h o) -> p h o", o=1).broadcast_to([P, HH, BOX]),
                                               box[:, c, sign:sign + 1, :].broadcast_to([P, HH, BOX]), ALU.mult)
                last.then_inc(m_open, 1)
                for sign in range(2):
                    V.tensor_reduce(m_size[:, sign, :], box[:, :, sign, 0:NC], axis=AX.X, op=ALU.max, apply_absolute_value=True)
                link.then(V.tensor_reduce(m_size[:, 2, :], a_qabs[:, :, :], axis=AX.X, op=ALU.max))
                link.then(V.tensor_tensor(m_size[:, 3, :], m_size[:, 0, :], m_size[:, 1, :], ALU.max))
                link.then(V.scalar_tensor_tensor(m_size[:, 0, :], m_size[:, 3, :], MAX_SLACK / MAX_SIZE, m_size[:, 2, :], ALU.mult, ALU.mult))
                link.then(V.tensor_reduce(m_crit[:, 1:2], m_size[:, 0, :], axis=AX.X, op=ALU.max))
                return link

            def m_evacuate(link, m, i, bank=aux):
                wait_alone(dve, m_product, m * M_STEPS + i + 1, dve_passed)
                if i < 8:
                    bound = bank[:, 0:2 * NS * BOX].rearrange("p (h k) -> p h k", k=BOX)
                    cols = m_cols[:, 2 * i:2 * i + 2, :].rearrange("p i h -> p (i h)")
                    link.then(V.tensor_reduce(cols, bound[:, :, 0:NC], axis=AX.X, op=ALU.max))
                    V.tensor_tensor(m_slack[:, i * 2 * NS:(i + 1) * 2 * NS], cols, bound[:, :, NC], ALU.subtract).then_inc(m_evacuated, 1)
                    if i == 7:
                        wait_alone(dve, m_evacuated, m * M_STEPS + 8, dve_passed)
                        link.then(V.tensor_reduce(m_crit[:, 2:3], m_slack[:, :], axis=AX.X, op=ALU.max))
                        V.tensor_tensor(m_crit[:, 0:1], m_crit[:, 1:2], m_crit[:, 2:3], ALU.max).then_inc(m_crit_done, 1)
                elif i == 8:
                    V.tensor_reduce(m_worst[:, :], aux[0:1, 0:P], axis=AX.X, op=ALU.max).then_inc(m_evacuated, 1)
                    wait_alone(dve, m_evacuated, m * M_STEPS + 9, dve_passed)
                    V.tensor_scalar(m_flag[:, :], m_worst[:, :], MAX_SLACK, None, ALU.is_gt).then_inc(m_flag_set, 1)
                else:
                    V.tensor_scalar(m_rows, aux[0:NS, :], -1.0, HEADROOM, ALU.mult, ALU.add).then_inc(m_evacuated, 1)
                    wait_alone(dve, m_evacuated, m * M_STEPS + i + 1, dve_passed)
                    maxima_parts(link, i - 9)
                    if i == M_STEPS - 1:
                        V.memset(m_mean[:, :], 0.0).then_inc(m_done, 1)

            def maxima_parts(link, k):
                at = slice(k * CH, (k + 1) * CH)
                link.then(V.tensor_copy(m_parts[:, 0, at], m_rows))
                link.then(V.tensor_tensor(m_rows, m_rows, m_parts[:, 0, at], ALU.subtract))
                link.then(V.tensor_copy(m_parts[:, 1, at], m_rows))
                link.then(V.tensor_tensor(m_parts[:, 2, at], m_rows, m_parts[:, 1, at], ALU.subtract))

            with dve.Fori(0, NC) as tc:
                for i in range(A_STEPS):
                    a_evacuate(tc, i, 0, tc, ps[:, i, :])
                    if i == 1:
                        with dve.If(tc < NC - 1):
                            a_stats(tc + 1)
                    if i == 2:
                        with dve.If(tc < NC - 1):
                            a_apply(tc + 1)
            link = m_prepare(0)
            for i in range(M_STEPS):
                m_evacuate(link, 0, i, ps[:, i % 8, :])
            assert link.count == M_LINKS, link.count

            exact_runs = dve.alloc_register("dve_exact_runs")
            dve.reg_mov(exact_runs, 0)
            with dve.Fori(0, B) as b:
                wait_alone(dve, m_flag_set, b + 1, dve_passed)
                exact = dve.value_load(m_flag[0:1, 0:1], min_val=0, max_val=1)
                with dve.If(exact > 0):
                    runs = dve.snap(exact_runs, min_val=0, max_val=B - 1)
                    with dve.Fori(0, NG) as g:
                        for n in range(4 * NB):
                            head, blk = n // NB, n % NB
                            shead = 2 * (head % 2) + head // 2
                            wait_alone(dve, m_scores, (runs * NG + g) * (4 * NB) + n + 1, dve_passed)
                            V.tensor_reduce(m_cols[:, blk, bass.ds(g * 4 + shead, 1)], ps[:, 4 * (n % 2):4 * (n % 2) + 4, :], axis=AX.XY, op=ALU.max).then_inc(m_reduced, 1)
                    link = Chain(dve, exact_chain, runs * (P_LINKS * NC), dve_passed)
                    wait_alone(dve, m_stored, (b + 1) * DMA, dve_passed)
                    for k in range(NC):
                        wait_alone(dve, exact_product, runs * NC + k + 1, dve_passed)
                        V.tensor_scalar(m_rows, aux[0:NS, :], -1.0, HEADROOM, ALU.mult, ALU.add).then_inc(exact_evacuated, 1)
                        wait_alone(dve, exact_evacuated, runs * NC + k + 1, dve_passed)
                        maxima_parts(link, k)
                    V.memset(m_mean[:, :], 0.0).then_inc(exact_done, 1)
                    wait_alone(dve, exact_done, runs + 1, dve_passed)
                    dve.reg_add(exact_runs, exact_runs, 1)

                with dve.Fori(0, GP) as gp:
                    body = b * GP + gp
                    ejob = (body + (B - 1) * GP) % (B * GP)
                    with dve.If(b < B - 1):
                        a_stats(body + NC)
                        a_apply(body + NC)
                    for s in range(SEGS):
                        if s == 3:
                            with dve.If(b < B - 1):
                                with dve.If(gp == GP - 1):
                                    link = m_prepare(b + 1)
                        for i in (2 * s, 2 * s + 1):
                            if i < A_STEPS:
                                with dve.If(b < B - 1):
                                    a_evacuate(body + NC, i, b + 1, gp)
                            elif i < A_STEPS + E_STEPS:
                                with dve.If(b > 0):
                                    e_evacuate(ejob, i - A_STEPS, b - 1)
                            if i % 2 == 0 and s in M_GROUPS:
                                with dve.If(b < B - 1):
                                    with dve.If(gp == GP - 1):
                                        if s == 6:
                                            wait_alone(dve, m_stored, (b + 1) * DMA, dve_passed)
                                        for k in M_GROUPS[s]:
                                            m_evacuate(link, b + 1, k)
                            if i == 13:
                                with dve.If(b < B - 1):
                                    with dve.If(gp == GP - 1):
                                        m_evacuate(link, b + 1, 11)
                        if s == 7:
                            with dve.If(b < B - 1):
                                with dve.If(gp == GP - 1):
                                    m_evacuate(link, b + 1, 12)
                        segment(body, s)

            link = Chain(dve, e_chain, LAST_JOB * E_LINKS)
            for k, (tc, i) in enumerate(LAST_E):
                e_evacuate(LAST_JOB + tc, i, B - 1, (aux, pv)[k % 2], k, link, (e_x2, a_x)[tc % 2])


_OUTS = [((4, 2048, 256), "float32")]


def kernel(**inputs):
    import concourse.bacc as _bacc
    from concourse.bass_utils import run_bass_kernel_spmd as _run

    nc = _bacc.Bacc("TRN2", target_bir_lowering=False, num_devices=1)
    plain = {k: np.asarray(v) for k, v in inputs.items()}
    laid = [
        ("x", plain["L0_attn_query"]),
        ("wqT", plain["L0_attn_Wq"].T), ("wkT", plain["L0_attn_Wk"].T), ("wvT", plain["L0_attn_Wv"].T), ("woT", plain["L0_attn_Wo"].T),
        ("lq1", plain["L0_attn_lambda_q1"]), ("lk1", plain["L0_attn_lambda_k1"]),
        ("lq2", plain["L0_attn_lambda_q2"]), ("lk2", plain["L0_attn_lambda_k2"]),
        ("subln", plain["L0_attn_subln_w"]), ("wfT", plain["L0_ffn_weight"].T),
        ("cT", plain["L0_c"].T), ("wmod", plain["L0_wmod"]),
    ]
    arrays, args = {}, []
    for name, a in laid:
        a = np.ascontiguousarray(a)
        arrays[f"in_{name}_dram"] = a
        args.append(nc.dram_tensor(f"in_{name}_dram", a.shape, mybir.dt.from_np(a.dtype), kind="ExternalInput").ap())
    for i, (shape, dtype) in enumerate(_OUTS):
        args.append(nc.dram_tensor(f"out_{i}_dram", shape, mybir.dt.from_np(np.dtype(dtype)), kind="ExternalOutput").ap())
    adaln_diff_attention(nc, *args)
    r = _run(nc, [arrays], core_ids=[0])
    return r.results[0]["out_0_dram"]
```
